# Optimizing a Trainium2 kernel written in Bass

```python
import numpy as np
import jax
import jax.numpy as jnp

def _softmax(x, axis=-1):
    return jax.nn.softmax(x, axis=axis)

def _gelu(x):
    return jax.nn.gelu(x, approximate=True)

def _silu(x):
    return jax.nn.silu(x)

def _sigmoid(x):
    return jax.nn.sigmoid(x)

def _layernorm(x, axis=-1, eps=1e-05):
    m = jnp.mean(x, axis=axis, keepdims=True)
    v = jnp.var(x, axis=axis, keepdims=True)
    return (x - m) / jnp.sqrt(v + eps)

def _scatter_add(tgt, idx, src, axis=0):
    return tgt.at[idx].add(src)

def _segment_sum(src, seg, n):
    return jax.ops.segment_sum(src, seg, n)
kernel_name = 'mk_adj_resnorm_d2_adj_r2_7dd7e8'

def setup_inputs(seed: int=0):
    np.random.seed(seed)
    _w = jnp.asarray

    def _rec_inputs():
        import jax
        import jax.numpy as jnp
        _gk = jax.random.key(seed)
        x = -8.015e-05 + 0.9999 * jax.random.normal(jax.random.fold_in(_gk, 1), (64, 128, 128), jnp.float32)
        _w = (1.0 + jnp.arange(128, dtype=jnp.float32)) ** (-0.5)
        _w = _w / _w.mean()
        _pij = jnp.clip(0.0625 * _w[:, None] * _w[None, :], 0.0, 1.0)
        _a = jax.random.uniform(jax.random.fold_in(_gk, 2), (64, 128, 128)) < _pij
        _a = jnp.logical_or(_a, jnp.swapaxes(_a, -1, -2))
        _a = jnp.logical_or(_a, jnp.eye(128, dtype=bool))
        _af = _a.astype(jnp.float32)
        _af = _af * jax.random.uniform(jax.random.fold_in(_gk, 3), (64, 128, 128), jnp.float32, 0.05, 0.999837)
        adj = _af
        _nm = jnp.ones((64, 128), dtype=bool)
        nodemask = jnp.where(_nm, 1.0, 0.0).astype(jnp.float32)
        return (x, adj, nodemask)
    x, adj, nodemask = _rec_inputs()

    def _L0_gnn_setup():
        import jax, jax.numpy as jnp
        import numpy as np
        GROUPS = [list(range(25)), [0, 1, 2, 3, 4, 5, 6, 7, 8], [0, 9, 10, 11, 12, 13, 14], [6, 7, 8, 12, 13, 14], [3, 4, 5, 9, 10, 11]]
        B, N, D_IN, D_HID = (4096, 25, 128, 256)

        def _graph_conv(x, adj, W, b):
            n = adj.shape[-1]
            A = adj + jnp.eye(n, dtype=adj.dtype)
            deg = jnp.sum(A, axis=-1)
            deg_safe = jnp.where(deg == 0, 1.0, deg)
            dinv = jnp.where(deg == 0, 0.0, deg_safe ** (-0.5))
            norm_adj = dinv[:, :, None] * A * dinv[:, None, :]
            support = jnp.einsum('bnd,de->bne', x, W)
            out = jnp.einsum('bnm,bme->bne', norm_adj, support) + b
            return jax.nn.relu(out)
        key = jax.random.key(seed)
        ks = jax.random.split(key, 7)
        s1 = float(np.sqrt(6.0 / (D_IN + D_HID)))
        s2 = float(np.sqrt(6.0 / (D_HID + D_IN)))
        return {'x': jax.random.normal(ks[0], (B, N, D_IN), dtype=jnp.float32), 'adj': jax.random.uniform(ks[1], (B, N, N), dtype=jnp.float32), 'W1': jax.random.uniform(ks[2], (5, D_IN, D_HID), jnp.float32, -s1, s1), 'b1': jnp.zeros((5, D_HID), dtype=jnp.float32), 'W2': jax.random.uniform(ks[3], (5, D_HID, D_IN), jnp.float32, -s2, s2), 'b2': jnp.zeros((5, D_IN), dtype=jnp.float32), 'fusion_w': jnp.ones((5,), dtype=jnp.float32)}
    _L0_gnn_all = _L0_gnn_setup()
    _L0_gnn_in = {k: v for k, v in _L0_gnn_all.items() if k in ('W1', 'b1', 'W2', 'b2', 'fusion_w')}
    del _L0_gnn_all

    def _L1_gnn_setup():
        import jax, jax.numpy as jnp
        import numpy as np
        B, N, D, C, L = (64, 256, 128, 128, 5)
        EDGE_P = 0.02

        def _gru_cell(m, h, w_ih, w_hh, b_ih, b_hh):
            gi = m @ w_ih.T + b_ih
            gh = h @ w_hh.T + b_hh
            i_r, i_z, i_n = jnp.split(gi, 3, axis=-1)
            h_r, h_z, h_n = jnp.split(gh, 3, axis=-1)
            r = jax.nn.sigmoid(i_r + h_r)
            z = jax.nn.sigmoid(i_z + h_z)
            n = jnp.tanh(i_n + r * h_n)
            return (1.0 - z) * n + z * h
        key = jax.random.key(seed)
        ks = jax.random.split(key, 8)
        x = jax.random.normal(ks[0], (B, N, D), dtype=jnp.float32)
        adj = (jax.random.uniform(ks[1], (B, N, N)) < EDGE_P).astype(jnp.float32)
        mask = jnp.ones((B, N), dtype=jnp.float32)
        s = 1.0 / np.sqrt(C).astype(np.float32)
        weight = jax.random.uniform(ks[2], (L, C, C), minval=-s, maxval=s, dtype=jnp.float32)
        w_ih = jax.random.uniform(ks[3], (3 * C, C), minval=-s, maxval=s, dtype=jnp.float32)
        w_hh = jax.random.uniform(ks[4], (3 * C, C), minval=-s, maxval=s, dtype=jnp.float32)
        b_ih = jax.random.uniform(ks[5], (3 * C,), minval=-s, maxval=s, dtype=jnp.float32)
        b_hh = jax.random.uniform(ks[6], (3 * C,), minval=-s, maxval=s, dtype=jnp.float32)
        return dict(x=x, adj=adj, mask=mask, weight=weight, w_ih=w_ih, w_hh=w_hh, b_ih=b_ih, b_hh=b_hh)
    _L1_gnn_all = _L1_gnn_setup()
    _L1_gnn_in = {k: v for k, v in _L1_gnn_all.items() if k in ('weight', 'w_ih', 'w_hh', 'b_ih', 'b_hh')}
    del _L1_gnn_all
    return {'x': x, 'adj': adj, 'nodemask': nodemask, 'L0_gnn_W1': _L0_gnn_in['W1'], 'L0_gnn_b1': _L0_gnn_in['b1'], 'L0_gnn_W2': _L0_gnn_in['W2'], 'L0_gnn_b2': _L0_gnn_in['b2'], 'L0_gnn_fusion_w': _L0_gnn_in['fusion_w'], 'L1_gnn_weight': _L1_gnn_in['weight'], 'L1_gnn_w_ih': _L1_gnn_in['w_ih'], 'L1_gnn_w_hh': _L1_gnn_in['w_hh'], 'L1_gnn_b_ih': _L1_gnn_in['b_ih'], 'L1_gnn_b_hh': _L1_gnn_in['b_hh']}

def reference(x, adj, nodemask, L0_gnn_W1, L0_gnn_b1, L0_gnn_W2, L0_gnn_b2, L0_gnn_fusion_w, L1_gnn_weight, L1_gnn_w_ih, L1_gnn_w_hh, L1_gnn_b_ih, L1_gnn_b_hh):
    import jax
    import jax.numpy as jnp

    def _L0_gnn_ref(x, adj, W1, b1, W2, b2, fusion_w):
        import jax, jax.numpy as jnp
        import numpy as np
        GROUPS = [list(range(25)), [0, 1, 2, 3, 4, 5, 6, 7, 8], [0, 9, 10, 11, 12, 13, 14], [6, 7, 8, 12, 13, 14], [3, 4, 5, 9, 10, 11]]
        B, N, D_IN, D_HID = (4096, 25, 128, 256)

        def _graph_conv(x, adj, W, b):
            n = adj.shape[-1]
            A = adj + jnp.eye(n, dtype=adj.dtype)
            deg = jnp.sum(A, axis=-1)
            deg_safe = jnp.where(deg == 0, 1.0, deg)
            dinv = jnp.where(deg == 0, 0.0, deg_safe ** (-0.5))
            norm_adj = dinv[:, :, None] * A * dinv[:, None, :]
            support = jnp.einsum('bnd,de->bne', x, W)
            out = jnp.einsum('bnm,bme->bne', norm_adj, support) + b
            return jax.nn.relu(out)
        norm_w = jax.nn.softmax(fusion_w)
        fused = jnp.zeros_like(x)
        for g, idx_list in enumerate(GROUPS):
            idx = jnp.asarray(idx_list)
            x_g = x[:, idx, :]
            adj_g = adj[:, idx][:, :, idx]
            h = _graph_conv(x_g, adj_g, W1[g], b1[g])
            out_g = _graph_conv(h, adj_g, W2[g], b2[g])
            fused = fused.at[:, idx, :].add(norm_w[g] * out_g)
        return fused

    def _L1_gnn_ref(x, adj, mask, weight, w_ih, w_hh, b_ih, b_hh):
        import jax, jax.numpy as jnp
        import numpy as np
        B, N, D, C, L = (64, 256, 128, 128, 5)
        EDGE_P = 0.02

        def _gru_cell(m, h, w_ih, w_hh, b_ih, b_hh):
            gi = m @ w_ih.T + b_ih
            gh = h @ w_hh.T + b_hh
            i_r, i_z, i_n = jnp.split(gi, 3, axis=-1)
            h_r, h_z, h_n = jnp.split(gh, 3, axis=-1)
            r = jax.nn.sigmoid(i_r + h_r)
            z = jax.nn.sigmoid(i_z + h_z)
            n = jnp.tanh(i_n + r * h_n)
            return (1.0 - z) * n + z * h
        A = (adj != 0).astype(x.dtype)
        h = x
        for l in range(weight.shape[0]):
            m = jnp.einsum('bnd,de->bne', h, weight[l])
            agg = jnp.einsum('bij,bid->bjd', A, m)
            h = _gru_cell(agg, h, w_ih, w_hh, b_ih, b_hh)
        return h * mask[..., None]
    x = _layernorm(x + _L0_gnn_ref(x, adj, L0_gnn_W1, L0_gnn_b1, L0_gnn_W2, L0_gnn_b2, L0_gnn_fusion_w), axis=-1)
    x = _layernorm(x + _L1_gnn_ref(x, adj, nodemask, L1_gnn_weight, L1_gnn_w_ih, L1_gnn_w_hh, L1_gnn_b_ih, L1_gnn_b_hh), axis=-1)
    return x

_drawn_inputs = setup_inputs


def setup_inputs(seed=0):
    import zlib

    import numpy as np

    out = dict(_drawn_inputs(seed))
    spreads = {'L0_gnn_b1': (0.0, 0.1), 'L0_gnn_b2': (0.0, 0.1), 'L0_gnn_fusion_w': (1.0, 0.2)}
    factors = {}
    for name, (base, spread) in spreads.items():
        noise = np.random.default_rng([zlib.crc32(name.encode()), seed]).standard_normal(out[name].shape)
        drawn = base * np.exp(spread * noise) if base else spread * noise
        out[name] = jnp.asarray(drawn.astype(out[name].dtype))
    for name, factor in factors.items():
        out[name] = (out[name] * factor).astype(out[name].dtype)
    return out
```

```python
import concourse.bass as bass
from concourse import mybir
from contextlib import ExitStack

B, N, D = 64, 128, 128
GROUPS = [list(range(25)), [0, 1, 2, 3, 4, 5, 6, 7, 8], [0, 9, 10, 11, 12, 13, 14],
          [6, 7, 8, 12, 13, 14], [3, 4, 5, 9, 10, 11]]
NG = len(GROUPS)
FN = 25
HID = 256
HC = HID // 128
LAYERS = 5
GATES = 3 * D
EPS = 1e-5

CB = 16
CHUNKS = B // CB
SB = 4
SLOTS = CB // SB
COLS = SB * N
STEPS = LAYERS * SLOTS

TILES = [(0, 4, b) for b in range(0, CB, 4)] + [(1, 8, 0), (1, 8, 8)] + [(g, 16, 0) for g in (2, 3, 4)]
NT = len(TILES)
ROWS = [len(GROUPS[g]) * k for g, k, _ in TILES]
TA = [t for t in range(NT) if TILES[t][0] == 0]
TB = [t for t in range(NT) if TILES[t][0] != 0]
OFF = {}
for half in (TA, TB):
    at = 0
    for t in half:
        OFF[t] = at
        at += ROWS[t]
COLS_A, COLS_B = sum(ROWS[t] for t in TA), sum(ROWS[t] for t in TB)


def runs(nodes):
    out = []
    for i, v in enumerate(nodes):
        if out and v == out[-1][1] + out[-1][2]:
            out[-1][2] += 1
        else:
            out.append([i, v, 1])
    return [tuple(r) for r in out]


class Window:

    def __init__(self, sg, l, slot, turn, feed, enter, ready=None, apply=None):
        self.sg, self.l, self.slot, self.turn, self.feed, self.enter = sg, l, slot, turn, feed, enter
        self.ready, self.apply = ready, apply
        self.k = sg * STEPS + l * SLOTS + slot
        self.visit = sg * SLOTS + slot - 1
        self.prev = (slot - 1) % SLOTS
        self.turned = sg * (STEPS - SLOTS) + l * SLOTS + slot - 1


def opening(sg, first):
    return Window(sg, 0, 0, None if first else "leave", False, not first)


def supergroup(eng, sg, more):
    norms = {1: (0, None), 2: (1, 0), 3: (None, 1)}
    late = {0: (2, None), 1: (3, 2), 2: (None, 3), 3: (None, None)}
    for slot in range(1, SLOTS):
        yield Window(sg, 0, slot, "step", slot >= 2, False, *(norms[slot] if more else ()))
    with eng.Fori(1, LAYERS - 1) as l:
        for slot in range(SLOTS):
            yield Window(sg, l, slot, "step", True, False)
    for slot in range(SLOTS):
        yield Window(sg, LAYERS - 1, slot, "leave" if slot else "step", slot < 2, more and slot > 0,
                     *(late[slot] if more else ()))


def windows(eng):
    yield opening(0, True)
    with eng.Fori(0, CHUNKS - 1) as sg:
        yield from supergroup(eng, sg, True)
        yield opening(sg + 1, False)
    yield from supergroup(eng, CHUNKS - 1, False)
    yield None


def build(nc, x, adj, nodemask, W1, b1, W2, b2, fusion_w, weight, w_ih, w_hh, b_ih, b_hh, out):
    f32, f32r = mybir.dt.float32, mybir.dt.float32r
    ALU, ACT, AX = mybir.AluOpType, mybir.ActivationFunctionType, mybir.AxisListType
    ctx = ExitStack()
    with ctx:
        ctx.enter_context(nc.allow_non_contiguous_dma(reason="small rows of the adjacency"))

        def sb(name, shape, dt=f32):
            return ctx.enter_context(nc.sbuf_tensor(name, shape, dt))

        def sem(name):
            return ctx.enter_context(nc.semaphore(name))

        xn = sb("xn", [128, B, D])
        an = sb("an", [128, B, N])
        ident = sb("ident", [128, 128])
        w1 = sb("w1", [128, NG, HID])
        w2 = sb("w2", [128, NG, HC, D])
        rows = sb("rows", [NG * HC + NG + 6, 128])
        biasc = sb("biasc", [128, NG * HC + NG + 6])
        maskr = sb("maskr", [B, N])
        maskc = sb("maskc", [128, B])
        wh = sb("wh", [128, 2, GATES], f32r)
        wf = sb("wf", [128, LAYERS, 2, GATES], f32r)
        wcur = sb("wcur", [128, 2, GATES], f32r)
        gb = sb("gb", [128, 2])
        fw = sb("fw", [128, NG])
        fmx = sb("fmx", [128, 1])
        fsum = sb("fsum", [128, 1])
        fb2 = sb("fb2", [128, NG])
        ac = sb("ac", [128, CHUNKS, NT, FN])
        member = sb("member", [128, NT, FN])
        unit = sb("unit", [128, NT, FN])
        ksel = {k: sb(f"ksel{k}", [128, k]) for k in (4, 8, 16)}
        deg = sb("deg", [128, CHUNKS, NT])
        zero = sb("zero", [128, CHUNKS, NT])
        dinv = sb("dinv", [128, CHUNKS, NT])
        half = sb("half", [128, CHUNKS * NT])
        xt = sb("xt", [128, NT, D])
        bda = sb("bda", [128, COLS_A])
        bdb = sb("bdb", [128, COLS_B])
        na = sb("na", [128, COLS_A])
        nb = sb("nb", [128, COLS_B])
        ya = sb("ya", [128, COLS_A])
        yb = sb("yb", [128, COLS_B])
        ha = sb("ha", [128, HC, COLS_A])
        hb = sb("hb", [128, HC, COLS_B])
        s2 = sb("s2", [128, NT, D])
        fused = sb("fused", [128, CB * FN + 128])
        part = sb("part", [128, COLS_B])
        hT = sb("hT", [128, SLOTS, COLS])
        hhi = sb("hhi", [128, SLOTS, COLS], f32r)
        hlo = sb("hlo", [128, SLOTS, COLS], f32r)
        nat = sb("nat", [128, SLOTS, SB, D])
        ghi = sb("ghi", [128, SLOTS, COLS], f32r)
        glo = sb("glo", [128, SLOTS, COLS], f32r)
        rg = sb("rg", [128, 2, COLS])
        zg = sb("zg", [128, 2, COLS])
        cg = sb("cg", [128, 2, COLS])
        ng = sb("ng", [128, 2, COLS])
        dg = sb("dg", [128, 2, COLS])
        wir = rg[:, 0, 0:GATES].rearrange("p (c d) -> p c d", c=3)
        whr = rg[:, 1, 0:GATES].rearrange("p (c d) -> p c d", c=3)
        wl = zg[:].rearrange("p o (l d) -> p (o l) d", d=D)[:, 0:LAYERS, :]
        wlt = cg[:].rearrange("p o (l d) -> p (o l) d", d=D)[:, 0:LAYERS, :]
        wit = ng[:, 0, 0:GATES]
        yo = sb("yo", [128, 2, SB, D])
        st1, ag1, rs1, nm1 = sb("st1", [128, SB, 6]), sb("ag1", [128, SB, 2]), sb("rs1", [128, SB]), sb("nm1", [128, SB])
        st2, ag2, rs2, nm2 = sb("st2", [128, SB, 6]), sb("ag2", [128, 2, SB, 2]), sb("rs2", [128, 2, SB]), sb("nm2", [128, 2, SB])

        P = [ctx.enter_context(nc.psum_tensor(f"p{i}", [128, 512], f32)) for i in range(8)]
        PR, PH, PZ, PI, PT, PX = P[:6]
        PG = P[6:8]

        def b1c(g, c):
            return biasc[:, g * HC + c:g * HC + c + 1]
        BI = NG * HC + NG
        bin_, bhn = biasc[:, BI + 2:BI + 3], biasc[:, BI + 5:BI + 6]

        (w_in, wl_in, st_in, ac_in, xt_in, xa_in) = map(sem, ("w_in", "wl_in", "st_in", "ac_in", "xt_in", "xa_in"))
        ident_ok, ac_zero, dve_c, pool_c, exp_ok = map(sem, ("ident_ok", "ac_zero", "dve_c", "pool_c", "exp_ok"))
        prep_t, prep_a, prep_v, prep_f, prep_hi, prep_lo, fw_ok, b_ok = map(sem, (
            "prep_t", "prep_a", "prep_v", "prep_f", "prep_hi", "prep_lo", "fw_ok", "b_ok"))
        deg_ok, pow_ok, am_ok, bd_ok = map(sem, ("deg_ok", "pow_ok", "am_ok", "bd_ok"))
        t_ps, y_ps, h_ps, s_ps, o_ps, f_ps = map(sem, ("t_ps", "y_ps", "h_ps", "s_ps", "o_ps", "f_ps"))
        na_ok, nb_ok, ya_ok, yb_ok, ha_ok, hb_ok, sa_ok, sb_ok, oa_ok, ob_ok, fused_ok, x_ok, a_ok = map(sem, (
            "na_ok", "nb_ok", "ya_ok", "yb_ok", "ha_ok", "hb_ok", "sa_ok", "sb_ok", "oa_ok", "ob_ok", "fused_ok", "x_ok", "a_ok"))
        r_ps, i_ps, z_ps, T_ps, X_ps, F_ps, G_ps = map(sem, ("r_ps", "i_ps", "z_ps", "T_ps", "X_ps", "F_ps", "G_ps"))
        r_ok, z_ok, n_ok, t1_ok, c_ok, d_ok, e_ok, h_ok = map(sem, ("r_ok", "z_ok", "n_ok", "t1_ok", "c_ok", "d_ok", "e_ok", "h_ok"))
        hi_ok, lo_ok, nat_ok, ghi_ok, glo_ok, wcur_ok, hTx_ok = map(sem, (
            "hi_ok", "lo_ok", "nat_ok", "ghi_ok", "glo_ok", "wcur_ok", "hTx_ok"))
        bn1, ln1_st, ln1_rs, ln1_ok, x2_ok, sum_ok, bn2, ln2_st, ln2_rs, ln2_ok, out_ok = map(sem, (
            "bn1", "ln1_st", "ln1_rs", "ln1_ok", "x2_ok", "sum_ok", "bn2", "ln2_st", "ln2_rs", "ln2_ok", "out_ok"))
        yo_free, gathered, dev1, dev2 = map(sem, ("yo_free", "gathered", "dev1", "dev2"))
        waited = sem("waited")

        block = ctx.enter_context(nc.Block())

        def tile_rows(dram, c, t):
            g, k, b0 = TILES[t]
            for i, v, n in runs(GROUPS[g]):
                yield i * k, n * k, dram[bass.ds(c * CB + b0, k), v:v + n, :].rearrange("k n d -> n k d")

        def load_chunk(eng, c):
            for dst, src in ((xn, x), (an, adj)):
                for b in (0, CB // 2):
                    eng.dma_start(dst[:, bass.ds(c * CB + b, CB // 2), :],
                                  src[bass.ds(c * CB + b, CB // 2), :, :].rearrange("b n d -> n b d")).then_inc(xa_in, 16)

        def group_cols(g):
            mine = [t for t in TB if TILES[t][0] == g]
            return OFF[mine[0]], OFF[mine[-1]] + ROWS[mine[-1]]

        ADDS = sum(len(runs(GROUPS[TILES[t][0]])) for t in TB)
        N_RUNS = sum(len(runs(GROUPS[g])) for g, _, _ in TILES)

        @block.sync
        def _(sp):
            sp.wait_ge(ac_zero, 1)
            for c in range(CHUNKS):
                for t in range(NT):
                    for r0, n, src in tile_rows(adj, c, t):
                        sp.dma_start(ac[r0:r0 + n, c, t, :], src[:, :, 0:FN]).then_inc(ac_in, 16)
                if c == 0:
                    for t in range(NT):
                        for r0, n, src in tile_rows(x, 0, t):
                            sp.dma_start(xt[r0:r0 + n, t, :], src).then_inc(xt_in, 16)
            with sp.Fori(1, CHUNKS) as c:
                sp.wait_ge(xa_in, 64 * c)
                load_chunk(sp, c)
                sp.wait_ge(y_ps, 2 * c)
                for t in range(NT):
                    for r0, n, src in tile_rows(x, c, t):
                        sp.dma_start(xt[r0:r0 + n, t, :], src).then_inc(xt_in, 16)
            sp.sem_inc(yo_free, 2)
            with sp.Fori(0, B // SB // 2) as pair:
                for o in range(2):
                    v = 2 * pair + o
                    sp.wait_ge(ln2_ok, v + 1)
                    sp.dma_start(out[bass.ds(v * SB, SB), :, :].rearrange("b n d -> n b d"),
                                 yo[:, o, :, :]).then_inc(out_ok, 16)
                    sp.wait_ge(out_ok, 16 * (v + 1))
                    sp.sem_inc(yo_free, 1)
            sp.wait_ge(out_ok, 16 * (B // SB))

        def wait_alone(eng, signal, value):
            eng.wait_ge(signal, value)
            eng.sem_inc(waited, 1)

        def counter(eng, signal):
            n = [0]

            def link(ins):
                n[0] += 1
                ins.then_inc(signal, 1)
                eng.wait_ge(signal, n[0])
            return link

        @block.gpsimd
        def _(pool):
            link = counter(pool, pool_c)
            link(nc.gpsimd.memset(ident[:], 0.0))
            nc.gpsimd.affine_select(out=ident[:], in_=ident[:], compare_op=ALU.not_equal, fill=1.0, base=0,
                                    pattern=[[-1, 128]], channel_multiplier=1).then_inc(ident_ok, 1)
            nc.gpsimd.memset(ac[:], 0.0).then_inc(ac_zero, 1)
            nc.gpsimd.memset(fused[:], 0.0)
            link(nc.gpsimd.memset(half[:], -0.5))
            pool.wait_ge(deg_ok, 1)
            nc.gpsimd.tensor_tensor(dinv[:].rearrange("p c t -> p (c t)"), deg[:].rearrange("p c t -> p (c t)"),
                                    half[:], ALU.pow).then_inc(pow_ok, 1)

            def spread(c):
                last = None
                for t0, nt, pieces in ((0, 4, [(0, 0, 1, 25)]), (4, 2, [(0, 0, 1, 9)]), (6, 1, [(0, 0, 1, 1), (1, 9, 1, 6)]),
                                       (7, 1, [(0, 6, 2, 3)]), (8, 1, [(0, 3, 2, 3)])):
                    k, r, o = TILES[t0][1], ROWS[t0], OFF[t0]
                    dst = bda if t0 == 0 else bdb
                    am = ac[0:r, bass.ds(c, 1), t0:t0 + nt, :].rearrange("p o t m -> p (o t) m")
                    for i, v, s, n in pieces:
                        src = am[:, :, v:v + n] if s == 1 else am[:, 0, v:v + 12].rearrange("p (s m) -> p s m", s=2)[:, :, 0:n]
                        a = nt * s
                        d = dst[0:r, o + i * k:o + i * k + a * n * k].rearrange("p (a m k) -> p a m k", a=a, k=k)
                        last = nc.gpsimd.tensor_tensor(
                            d, src.unsqueeze(3).to_broadcast([r, a, n, k]),
                            ksel[k][0:r, :].unsqueeze(1).unsqueeze(1).to_broadcast([r, a, n, k]), ALU.mult)
                last.then_inc(bd_ok, 1)

            def gather(c):
                pool.wait_ge(oa_ok, c + 1)
                pool.wait_ge(ob_ok, c + 1)
                f = fused[:, 0:CB * FN].rearrange("p (b n) -> p b n", n=FN)
                n_add = 0
                for t in TB:
                    g, k, b0 = TILES[t]
                    for i, v, n in runs(GROUPS[g]):
                        d = f[:, b0:b0 + k, v:v + n]
                        s = part[:, OFF[t] + i * k:OFF[t] + (i + n) * k].rearrange("p (n k) -> p k n", k=k)
                        if n_add:
                            pool.wait_ge(gathered, ADDS * c + n_add)
                        n_add += 1
                        last = nc.gpsimd.tensor_tensor(d, d, s, ALU.add).then_inc(gathered, 1)
                pool.wait_ge(gathered, ADDS * c + ADDS)
                pool.sem_inc(fused_ok, 1)

            pool.wait_ge(am_ok, 1)
            spread(0)
            with pool.Fori(0, CHUNKS - 1) as c:
                pool.wait_ge(t_ps, 2 * c + 2)
                spread(c + 1)
                gather(c)
            gather(CHUNKS - 1)

            def deviation(ag, rs, nm, done, visit):
                nc.gpsimd.tensor_scalar(rs, ag[:, :, 1], EPS, 1.0, ALU.add, ALU.mult).then_inc(done, 1)
                nc.gpsimd.tensor_scalar(nm, ag[:, :, 0], -1.0, 0.0, ALU.mult, ALU.add).then_inc(done, 1)
                pool.wait_ge(done, 3 * visit + 1)
                nc.gpsimd.tensor_tensor(rs, rs, half[:, 0:SB], ALU.pow).then_inc(done, 1)
                pool.wait_ge(done, 3 * visit + 3)
                return nc.gpsimd.tensor_tensor(nm, nm, rs, ALU.mult)

            def deviation1(visit):
                if not isinstance(visit, int) or visit:
                    pool.wait_ge(ln1_ok, visit)
                wait_alone(pool, ln1_st, visit + 1)
                deviation(ag1, rs1[:], nm1[:], dev1, visit).then_inc(ln1_rs, 1)

            for slot in range(SLOTS):
                deviation1(slot)
            for w in windows(pool):
                if w:
                    pool.wait_ge(n_ok, w.k + 1)
                    nc.gpsimd.tensor_tensor(dg[:, w.slot % 2, :], hT[:, w.slot, :], ng[:, w.slot % 2, :],
                                            ALU.subtract).then_inc(d_ok, 1)
                if w is None or w.turn == "leave":
                    visit, o = (B // SB - 1, (SLOTS - 1) % 2) if w is None else (w.visit, w.prev % 2)
                    wait_alone(pool, ln2_st, visit + 1)
                    deviation(ag2[:, o], rs2[:, o], nm2[:, o], dev2, visit).then_inc(ln2_rs, 1)
                if w and w.ready is not None:
                    deviation1((w.sg + 1) * SLOTS + w.ready)

        @block.scalar
        def _(act):
            for i, (name, src) in enumerate((("b1", b1.rearrange("g (c h) -> (g c) h", c=HC)), ("b2", b2),
                                             ("b_ih", b_ih.rearrange("(c h) -> c h", h=128)),
                                             ("b_hh", b_hh.rearrange("(c h) -> c h", h=128)))):
                r0 = (0, NG * HC, NG * HC + NG, NG * HC + NG + 3)[i]
                act.dma_start(rows[r0:r0 + src.shape[0], :], src).then_inc(w_in, 16)
            act.dma_start(maskr[:], nodemask).then_inc(w_in, 16)
            act.dma_start(fw[:], fusion_w.partition_broadcast(128)).then_inc(w_in, 16)
            act.dma_start(wir, w_ih.rearrange("(c e) d -> e c d", c=3)).then_inc(wl_in, 16)
            act.dma_start(whr, w_hh.rearrange("(c e) d -> e c d", c=3)).then_inc(wl_in, 16)
            act.dma_start(wl, weight.rearrange("l c e -> c l e")).then_inc(wl_in, 16)
            act.dma_start(w1[:], W1.rearrange("g d h -> d g h")).then_inc(st_in, 16)
            act.dma_start(w2[:], W2.rearrange("g (c h) d -> h g c d", c=HC)).then_inc(st_in, 16)
            load_chunk(act, 0)
            act.wait_ge(fw_ok, 1)
            nc.scalar.activation(fw[:], fw[:], ACT.Exp, bias=fmx[:], accum_out=fsum[:]).then_inc(exp_ok, 1)
            act.wait_ge(prep_t, 1)
            nc.scalar.copy(wit, P[0][:, 0:GATES])
            act.wait_ge(prep_t, 2)
            nc.scalar.copy(wh[:, 0, :], P[1][:, 0:GATES]).then_inc(prep_hi, 1)
            act.wait_ge(prep_t, 3)
            nc.scalar.copy(wlt[:, 0:4, :], P[2][:].rearrange("p (l d) -> p l d", l=4))
            act.wait_ge(prep_t, 4)
            nc.scalar.copy(wlt[:, 4, :], P[3][:, 0:128])
            nc.scalar.copy(maskc[:], P[3][:, 256:256 + B])
            nc.scalar.copy(biasc[:], P[3][:, 128:128 + NG * HC + NG + 6]).then_inc(prep_a, 1)
            for l in range(LAYERS):
                act.wait_ge(prep_f, l + 1)
                nc.scalar.copy(wf[:, l, 0, :], P[(4 + l) % 8][:, 0:GATES]).then_inc(prep_hi, 1)
            act.wait_ge(b_ok, 1)
            with act.Fori(0, CHUNKS) as c:
                act.wait_ge(t_ps, 2 * c + 1)
                for t in TA:
                    r, o = ROWS[t], OFF[t]
                    dv = dinv[0:r, bass.ds(c, 1), t:t + 1].rearrange("p o t -> p (o t)")
                    last = nc.scalar.activation(na[0:r, o:o + r], P[0][0:r, o:o + r], ACT.Identity, scale=dv)
                last.then_inc(na_ok, 1)
                act.wait_ge(y_ps, 2 * c + 1)
                nc.scalar.copy(ya[:], P[2][:, 0:COLS_A]).then_inc(ya_ok, 1)
                for h in range(HC):
                    act.wait_ge(h_ps, 4 * c + 1 + h)
                    nc.scalar.activation(ha[:, h, :], P[4 + h][:, 0:COLS_A], ACT.Relu, bias=b1c(0, h)).then_inc(ha_ok, 1)
                act.wait_ge(s_ps, 3 * c + 1)
                nc.scalar.copy(s2[0:ROWS[0], 0:4, :], P[0][0:ROWS[0], :].rearrange("p (t d) -> p t d", t=4)).then_inc(sa_ok, 1)
                act.wait_ge(o_ps, 2 * c + 1)
                nc.scalar.activation(fused[:, 0:CB * FN].rearrange("p (t k n) -> p t n k", t=4, n=FN),
                                     P[3][:, 0:COLS_A].rearrange("p (t n k) -> p t n k", t=4, n=FN),
                                     ACT.Relu, bias=fb2[:, 0:1], scale=fw[:, 0:1]).then_inc(oa_ok, 1)
                act.wait_ge(o_ps, 2 * c + 2)
                for g in range(1, NG):
                    a, b = group_cols(g)
                    last = nc.scalar.activation(part[:, a:b], P[4][:, a:b], ACT.Relu, bias=fb2[:, g:g + 1], scale=fw[:, g:g + 1])
                last.then_inc(ob_ok, 1)
            def aggregated(m, s, par):
                act.wait_ge(G_ps, m + 1)
                nc.scalar.copy(ghi[:, s, :], PG[par][:]).then_inc(ghi_ok, 1)

            def norm1(visit):
                act.wait_ge(ln1_rs, visit + 1)
                for q in range(SB):
                    xq = xn[:, bass.ds(visit * SB + q, 1), :].rearrange("p o d -> p (o d)")
                    last = nc.scalar.activation(xq, xq, ACT.Identity, bias=nm1[:, q:q + 1], scale=rs1[:, q:q + 1])
                last.then_inc(ln1_ok, 1)

            for s in range(SLOTS):
                norm1(s)
            for s in range(SLOTS):
                act.wait_ge(X_ps, s + 1)
                nc.scalar.copy(hT[:, s, :], PX[:])
                nc.scalar.copy(hhi[:, s, :], PX[:]).then_inc(hi_ok, 1)
                aggregated(s, s, s % 2)
            for w in windows(act):
                if w:
                    k, s, p = w.k, w.slot, w.slot % 2
                    if w.apply is not None:
                        norm1((w.sg + 1) * SLOTS + w.apply)
                    act.wait_ge(r_ps, k + 1)
                    nc.scalar.activation(rg[:, p, :], PR[:], ACT.Sigmoid, bias=gb[:, 0:1]).then_inc(r_ok, 1)
                    if w.turn == "step":
                        act.wait_ge(h_ok, k)
                        nc.scalar.copy(hhi[:, w.prev, :], hT[:, w.prev, :]).then_inc(hi_ok, 1)
                    act.wait_ge(z_ps, k + 1)
                    nc.scalar.activation(zg[:, p, :], PZ[:], ACT.Sigmoid, bias=gb[:, 1:2]).then_inc(z_ok, 1)
                    act.wait_ge(c_ok, k + 1)
                    nc.scalar.activation(ng[:, p, :], cg[:, p, :], ACT.Tanh, bias=bin_).then_inc(n_ok, 1)
                    if w.feed:
                        aggregated(k + 2, (s + 2) % SLOTS, s % 2)
                    if w.turn == "step":
                        act.wait_ge(T_ps, w.turned + 1)
                        nc.scalar.copy(nat[:, w.prev], PT[:].rearrange("p (b d) -> p b d", b=SB)).then_inc(nat_ok, 1)
                    if w.enter:
                        act.wait_ge(X_ps, w.visit + SLOTS + 1)
                        nc.scalar.copy(hT[:, w.prev, :], PX[:])
                        nc.scalar.copy(hhi[:, w.prev, :], PX[:]).then_inc(hi_ok, 1)
                        aggregated(k + 3, w.prev, (s + 3) % 2)
                if w is None or w.turn == "leave":
                    visit, o = (B // SB - 1, (SLOTS - 1) % 2) if w is None else (w.visit, w.prev % 2)
                    act.wait_ge(ln2_rs, visit + 1)
                    for q in range(SB):
                        last = nc.scalar.activation(yo[:, o, q, :], yo[:, o, q, :], ACT.Identity,
                                                    bias=nm2[:, o, q:q + 1], scale=rs2[:, o, q:q + 1])
                    last.then_inc(ln2_ok, 1)

        @block.vector
        def _(dve):
            link = counter(dve, dve_c)
            TT, TS, STT = nc.vector.tensor_tensor, nc.vector.tensor_scalar, nc.vector.scalar_tensor_tensor
            link(nc.vector.memset(member[:], 0.0))
            link(nc.vector.memset(unit[:], 0.0))
            dve.wait_ge(ident_ok, 1)
            for t, (g, k, _) in enumerate(TILES):
                for i, v, n in runs(GROUPS[g]):
                    nc.vector.memset(member[:, t, v:v + n], 1.0)
                    nc.vector.reduce_sum(unit[:, t, v:v + n],
                                         ident[:, i * k:(i + n) * k].rearrange("p (n k) -> p n k", k=k), AX.X)
            for k in ksel:
                last = nc.vector.reduce_sum(ksel[k][:], ident[:].rearrange("p (n k) -> p k n", k=k), AX.X)
            link(last)
            dve.wait_ge(w_in, 16 * 6)
            nc.vector.tensor_reduce(fmx[:], fw[:], AX.X, ALU.max, negate=True).then_inc(fw_ok, 1)
            dve.wait_ge(ac_in, 16 * N_RUNS * CHUNKS)
            flat = ac[:].rearrange("p c t m -> p c (t m)")

            def every(a):
                return a[:].rearrange("p t m -> p (t m)").unsqueeze(1).to_broadcast([128, CHUNKS, NT * FN])
            link(TT(flat, flat, every(member), ALU.mult))
            link(TT(flat, flat, every(unit), ALU.add))
            link(nc.vector.reduce_sum(deg[:], ac[:], AX.X))
            link(TS(zero[:], deg[:], 0.0, None, ALU.is_equal))
            TT(deg[:], deg[:], zero[:], ALU.add).then_inc(deg_ok, 1)
            link(TS(zero[:], zero[:], -1.0, 1.0, ALU.mult, ALU.add))
            dve.wait_ge(pow_ok, 1)
            link(TT(dinv[:], dinv[:], zero[:], ALU.mult))
            TT(ac[:], ac[:], dinv[:].unsqueeze(3).to_broadcast([128, CHUNKS, NT, FN]), ALU.mult).then_inc(am_ok, 1)
            dve.wait_ge(exp_ok, 1)
            link(nc.vector.reciprocal(fsum[:], fsum[:]))
            link(TS(fw[:], fw[:], fsum[:], None, ALU.mult))
            dve.wait_ge(prep_hi, 1)
            TT(wh[:, 1, :], P[1][:, 0:GATES], wh[:, 0, :], ALU.subtract)
            dve.wait_ge(prep_a, 1)
            TT(gb[:], biasc[:, BI:BI + 2], biasc[:, BI + 3:BI + 5], ALU.add)
            TT(fb2[:], biasc[:, NG * HC:BI], fw[:], ALU.mult).then_inc(b_ok, 1)
            for l in range(LAYERS):
                dve.wait_ge(prep_hi, l + 2)
                TT(wf[:, l, 1, :], P[(4 + l) % 8][:, 0:GATES], wf[:, l, 0, :], ALU.subtract).then_inc(prep_lo, 1)
            with dve.Fori(0, CHUNKS) as c:
                dve.wait_ge(t_ps, 2 * c + 2)
                for t in TB:
                    r, o = ROWS[t], OFF[t]
                    dv = dinv[0:r, bass.ds(c, 1), t:t + 1].rearrange("p o t -> p (o t)")
                    last = TS(nb[0:r, o:o + r], P[1][0:r, o:o + r], dv, None, ALU.mult)
                last.then_inc(nb_ok, 1)
                dve.wait_ge(y_ps, 2 * c + 2)
                nc.vector.tensor_copy(yb[:], P[3][:, 0:COLS_B]).then_inc(yb_ok, 1)
                for h in range(HC):
                    dve.wait_ge(h_ps, 4 * c + 3 + h)
                    for g in range(1, NG):
                        a, b = group_cols(g)
                        last = TS(hb[:, h, a:b], P[6 + h][:, a:b], b1c(g, h), 0.0, ALU.add, ALU.max)
                    last.then_inc(hb_ok, 1)
                dve.wait_ge(s_ps, 3 * c + 2)
                nc.vector.tensor_copy(s2[0:ROWS[4], 4:6, :], P[1][0:ROWS[4], 0:256].rearrange("p (t d) -> p t d", t=2))
                dve.wait_ge(s_ps, 3 * c + 3)
                nc.vector.tensor_copy(s2[0:ROWS[6], 6, :], P[2][0:ROWS[6], 0:128])
                nc.vector.tensor_copy(s2[0:ROWS[7], 7:9, :], P[2][0:ROWS[7], 128:384].rearrange("p (t d) -> p t d", t=2)).then_inc(sb_ok, 1)
                dve.wait_ge(xa_in, 64 * c + 64)
                ab = an[:, bass.ds(c * CB, CB), :]
                TS(ab, ab, 0.0, None, ALU.not_equal).then_inc(a_ok, 1)
                for q in range(4):
                    dve.wait_ge(f_ps, 4 * c + q + 1)
                    xq = xn[0:FN, bass.ds(c * CB + q * 4, 4), :]
                    TT(xq, xq, P[(5, 6, 7, 2)[q]][0:FN, :].rearrange("p (b d) -> p b d", b=4), ALU.add).then_inc(x_ok, 1)

            def end_step(k, s):
                dve.wait_ge(d_ok, k)
                TT(dg[:, s % 2, :], zg[:, s % 2, :], dg[:, s % 2, :], ALU.mult).then_inc(e_ok, 1)
                dve.wait_ge(e_ok, k)
                TT(hT[:, s, :], ng[:, s % 2, :], dg[:, s % 2, :], ALU.add).then_inc(h_ok, 1)

            def norm1(visit, b):
                for q in range(SB):
                    last = nc.vector.bn_stats(st1[:, q, :], xn[:, bass.ds(b + q, 1), :].rearrange("p o d -> p (o d)"))
                last.then_inc(bn1, 1)
                wait_alone(dve, bn1, visit + 1)
                for q in range(SB):
                    last = nc.vector.bn_aggr(ag1[:, q, :], st1[:, q, :])
                last.then_inc(ln1_st, 1)

            def settle(s, b, ready):
                wait_alone(dve, ln1_ok, ready)
                nc.vector.tensor_copy(nat[:, s], xn[:, bass.ds(b, SB), :]).then_inc(x2_ok, 1)

            def lo_state(m, s, src):
                dve.wait_ge(hi_ok, m + 1)
                TT(hlo[:, s, :], src, hhi[:, s, :], ALU.subtract).then_inc(lo_ok, 1)

            def lo_neighbours(m, s, par):
                dve.wait_ge(ghi_ok, m + 1)
                TT(glo[:, s, :], PG[par][:], ghi[:, s, :], ALU.subtract).then_inc(glo_ok, 1)

            dve.wait_ge(x_ok, 4 * CHUNKS)
            for s in range(SLOTS):
                if s:
                    dve.wait_ge(ln1_ok, s)
                norm1(s, s * SB)
            for s in range(SLOTS):
                settle(s, s * SB, s + 1)
            for s in range(SLOTS):
                lo_state(s, s, PX[:])
                lo_neighbours(s, s, s % 2)
            for w in windows(dve):
                if w:
                    k, s, p = w.k, w.slot, w.slot % 2
                    if s == 0:
                        if w.turn:
                            wait_alone(dve, z_ps, k)
                        nc.vector.tensor_copy(wcur[:], wf[:, bass.ds(w.l, 1)].rearrange("p o h e -> p (o h) e")).then_inc(wcur_ok, 1)
                    if w.enter:
                        dve.wait_ge(G_ps, k)
                        settle(w.prev, (w.visit + SLOTS) * SB, w.visit + SLOTS + 1)
                    if w.turn:
                        end_step(k, w.prev)
                    dve.wait_ge(r_ok, k + 1)
                    STT(cg[:, p, :], PH[:], bhn, rg[:, p, :], ALU.add, ALU.mult).then_inc(t1_ok, 1)
                    dve.wait_ge(i_ps, k + 1)
                    dve.wait_ge(t1_ok, k + 1)
                    TT(cg[:, p, :], cg[:, p, :], PI[:], ALU.add).then_inc(c_ok, 1)
                    if w.turn == "step":
                        lo_state(k + 3, w.prev, hT[:, w.prev, :])
                    if w.feed:
                        lo_neighbours(k + 2, (s + 2) % SLOTS, s % 2)
                    if w.ready is not None:
                        visit = (w.sg + 1) * SLOTS + w.ready
                        dve.wait_ge(ln1_ok, visit)
                        norm1(visit, visit * SB)
                else:
                    end_step(B // SB * LAYERS, SLOTS - 1)
                if w is None or w.turn == "leave":
                    visit, prev = (B // SB - 1, SLOTS - 1) if w is None else (w.visit, w.prev)
                    o = prev % 2
                    dve.wait_ge(F_ps, visit + 1)
                    dve.wait_ge(yo_free, visit + 1)
                    for q in range(SB):
                        b = visit * SB + q
                        last = STT(yo[:, o, q, :], PT[:, q * D:(q + 1) * D], maskc[:, bass.ds(b, 1)],
                                   xn[:, bass.ds(b, 1), :].rearrange("p o d -> p (o d)"), ALU.mult, ALU.add)
                    last.then_inc(sum_ok, 1)
                    dve.wait_ge(sum_ok, visit + 1)
                    for q in range(SB):
                        last = nc.vector.bn_stats(st2[:, q, :], yo[:, o, q, :])
                    last.then_inc(bn2, 1)
                    wait_alone(dve, bn2, visit + 1)
                    for q in range(SB):
                        last = nc.vector.bn_aggr(ag2[:, o, q, :], st2[:, q, :])
                    last.then_inc(ln2_st, 1)
                if w and w.enter:
                    lo_state(w.k + 3, w.prev, PX[:])
                    lo_neighbours(w.k + 3, w.prev, (w.slot + 3) % 2)

        @block.tensor
        def _(pe):
            MM, TR = nc.tensor.matmul, nc.tensor.transpose
            pe.wait_ge(ident_ok, 1)
            pe.wait_ge(wl_in, 48)
            for i in range(3):
                last = TR(P[0][:, i * 128:(i + 1) * 128], wir[:, i, :], ident[:])
            last.then_inc(prep_t, 1)
            for i in range(3):
                last = TR(P[1][:, i * 128:(i + 1) * 128], whr[:, i, :], ident[:])
            last.then_inc(prep_t, 1)
            for l in range(4):
                last = TR(P[2][:, l * 128:(l + 1) * 128], wl[:, l, :], ident[:])
            last.then_inc(prep_t, 1)
            TR(P[3][:, 0:128], wl[:, 4, :], ident[:])
            pe.wait_ge(w_in, 16 * 6)
            nr = NG * HC + NG + 6
            TR(P[3][:, 128:128 + nr], rows[:], ident[0:nr, 0:nr])
            TR(P[3][:, 256:256 + B], maskr[:], ident[0:B, 0:B]).then_inc(prep_t, 1)
            pe.wait_ge(prep_a, 1)
            for l in range(LAYERS):
                MM(P[(4 + l) % 8][:, 0:GATES], wlt[:, l, :], wit, start=True, stop=True).then_inc(prep_f, 1)
            pe.wait_ge(st_in, 32)
            pe.wait_ge(prep_lo, LAYERS)
            with pe.Fori(0, CHUNKS) as c:
                pe.wait_ge(bd_ok, c + 1)
                for half, bd, bank in ((TA, bda, 0), (TB, bdb, 1)):
                    for t in half:
                        r, o = ROWS[t], OFF[t]
                        last = TR(P[bank][0:r, o:o + r], bd[0:r, o:o + r], ident[0:r, 0:r])
                    last.then_inc(t_ps, 1)
                pe.wait_ge(xt_in, 16 * N_RUNS * (c + 1))
                pe.wait_ge(nb_ok, c + 1)
                for half, nn, bank, ready in ((TA, na, 2, na_ok), (TB, nb, 3, None)):
                    if ready:
                        pe.wait_ge(ready, c + 1)
                    for t in half:
                        r, o = ROWS[t], OFF[t]
                        last = MM(P[bank][:, o:o + r], xt[0:r, t, :], nn[0:r, o:o + r], start=True, stop=True)
                    last.then_inc(y_ps, 1)
                pe.wait_ge(ya_ok, c + 1)
                for h in range(HC):
                    MM(P[4 + h][:, 0:COLS_A], w1[:, 0, h * 128:(h + 1) * 128], ya[:], start=True, stop=True).then_inc(h_ps, 1)
                pe.wait_ge(yb_ok, c + 1)
                for h in range(HC):
                    for g in range(1, NG):
                        a, b = group_cols(g)
                        last = MM(P[6 + h][:, a:b], w1[:, g, h * 128:(h + 1) * 128], yb[:, a:b], start=True, stop=True)
                    last.then_inc(h_ps, 1)
                def second(tiles, hid, bank):
                    for i, t in enumerate(tiles):
                        g, r, o = TILES[t][0], ROWS[t], OFF[t]
                        for h in range(HC):
                            last = MM(P[bank][0:r, i * D:(i + 1) * D], hid[:, h, o:o + r], w2[:, g, h, :],
                                      start=(h == 0), stop=(h == HC - 1))
                    last.then_inc(s_ps, 1)
                pe.wait_ge(ha_ok, 2 * c + 2)
                second(TA, ha, 0)
                pe.wait_ge(hb_ok, 2 * c + 2)
                second(TB[0:2], hb, 1)
                second(TB[2:5], hb, 2)
                for half, nn, bank, ready in ((TA, na, 3, sa_ok), (TB, nb, 4, sb_ok)):
                    pe.wait_ge(ready, c + 1)
                    for t in half:
                        r, o = ROWS[t], OFF[t]
                        last = MM(P[bank][:, o:o + r], s2[0:r, t, :], nn[0:r, o:o + r], start=True, stop=True)
                    last.then_inc(o_ps, 1)
                pe.wait_ge(fused_ok, c + 1)
                for q in range(4):
                    for i in range(4):
                        b = 4 * q + i
                        last = TR(P[(5, 6, 7, 2)[q]][:, i * D:(i + 1) * D], fused[:, b * FN:b * FN + 128], ident[:])
                    last.then_inc(f_ps, 1)
            def turn(bank, src):
                for q in range(SB):
                    last = TR(bank[:, q * 128:(q + 1) * 128], src(q), ident[:])
                return last

            def aggregate(s, b, par):
                for q in range(SB):
                    last = MM(PG[par][:, q * N:(q + 1) * N], nat[:, s, q, :],
                              an[:, bass.ds(b + q, 1), :].rearrange("p o n -> p (o n)"), start=True, stop=True)
                last.then_inc(G_ps, 1)

            def product(bank, w, g, xhi, xlo, start, stop):
                cols = slice(g * D, (g + 1) * D)
                MM(bank[:], w[:, 0, cols], xhi, start=start, stop=False)
                MM(bank[:], w[:, 0, cols], xlo, start=False, stop=False)
                return MM(bank[:], w[:, 1, cols], xhi, start=False, stop=stop)

            pe.wait_ge(a_ok, CHUNKS)
            for s in range(SLOTS):
                pe.wait_ge(x2_ok, s + 1)
                if s:
                    pe.wait_ge(lo_ok, s)
                turn(PX, lambda q: nat[:, s, q, :]).then_inc(X_ps, 1)
                if s >= 2:
                    pe.wait_ge(glo_ok, s - 1)
                aggregate(s, s * SB, s % 2)
            for w in windows(pe):
                if w:
                    k, s = w.k, w.slot
                    xhi, xlo = hhi[:, s, :], hlo[:, s, :]
                    pe.wait_ge(hi_ok, k + 1)
                    pe.wait_ge(lo_ok, k + 1)
                    if w.turn:
                        pe.wait_ge(r_ok, k)
                    product(PR, wh, 0, xhi, xlo, True, False)
                    if w.turn:
                        pe.wait_ge(t1_ok, k)
                    product(PH, wh, 2, xhi, xlo, True, True)
                    if w.turn:
                        pe.wait_ge(z_ok, k)
                    product(PZ, wh, 1, xhi, xlo, True, False)
                    if s == 0:
                        pe.wait_ge(wcur_ok, w.sg * LAYERS + w.l + 1)
                    pe.wait_ge(ghi_ok, k + 1)
                    pe.wait_ge(glo_ok, k + 1)
                    xhi, xlo = ghi[:, s, :], glo[:, s, :]
                    product(PR, wcur, 0, xhi, xlo, False, True).then_inc(r_ps, 1)
                    if w.turn:
                        pe.wait_ge(c_ok, k)
                    product(PI, wcur, 2, xhi, xlo, True, True).then_inc(i_ps, 1)
                    product(PZ, wcur, 1, xhi, xlo, False, True).then_inc(z_ps, 1)
                    if w.feed:
                        pe.wait_ge(nat_ok, w.turned)
                        aggregate((s + 2) % SLOTS, w.sg * CB + (s + 2) % SLOTS * SB, s % 2)
                if w is None or w.turn:
                    k, prev = (B // SB * LAYERS, SLOTS - 1) if w is None else (w.k, w.prev)
                    pe.wait_ge(h_ok, k)
                    last = turn(PT, lambda q: hT[:, prev, q * 128:(q + 1) * 128])
                    last.then_inc(T_ps if w and w.turn == "step" else F_ps, 1)
                if w and w.enter:
                    pe.wait_ge(x2_ok, w.visit + SLOTS + 1)
                    pe.wait_ge(lo_ok, w.k + 3)
                    turn(PX, lambda q: nat[:, w.prev, q, :]).then_inc(X_ps, 1)
                    pe.wait_ge(glo_ok, w.k + 2)
                    aggregate(w.prev, (w.visit + SLOTS) * SB, (w.slot + 3) % 2)


_INS = ["x", "adj", "nodemask", "L0_gnn_W1", "L0_gnn_b1", "L0_gnn_W2", "L0_gnn_b2", "L0_gnn_fusion_w",
        "L1_gnn_weight", "L1_gnn_w_ih", "L1_gnn_w_hh", "L1_gnn_b_ih", "L1_gnn_b_hh"]


def kernel(**inputs):
    import numpy as _np
    import concourse.bacc as _bacc
    from concourse import mybir as _mybir
    from concourse.bass_utils import run_bass_kernel_spmd as _run

    nc = _bacc.Bacc("TRN2", target_bir_lowering=False, num_devices=1)
    arrays, args = {}, []
    for name in _INS:
        a = _np.ascontiguousarray(inputs[name])
        arrays[f"in_{name}_dram"] = a
        args.append(nc.dram_tensor(f"in_{name}_dram", a.shape, _mybir.dt.from_np(a.dtype), kind="ExternalInput").ap())
    args.append(nc.dram_tensor("out_0_dram", (B, N, D), _mybir.dt.float32, kind="ExternalOutput").ap())
    build(nc, *args)
    r = _run(nc, [arrays], core_ids=[0])
    return r.results[0]["out_0_dram"]
```

```python
import concourse.bass as bass
from concourse import mybir
from contextlib import ExitStack

B, N, D = 64, 128, 128
GROUPS = [list(range(25)), [0, 1, 2, 3, 4, 5, 6, 7, 8], [0, 9, 10, 11, 12, 13, 14],
          [6, 7, 8, 12, 13, 14], [3, 4, 5, 9, 10, 11]]
NG = len(GROUPS)
FN = 25
HID = 256
HC = HID // 128
LAYERS = 5
GATES = 3 * D
EPS = 1e-5

CB = 16
CHUNKS = B // CB
SB = 4
SLOTS = CB // SB
COLS = SB * N
STEPS = LAYERS * SLOTS

TILES = [(0, 4, b) for b in range(0, CB, 4)] + [(1, 8, 0), (1, 8, 8)] + [(g, 16, 0) for g in (2, 3, 4)]
NT = len(TILES)
ROWS = [len(GROUPS[g]) * k for g, k, _ in TILES]
TA = [t for t in range(NT) if TILES[t][0] == 0]
TB = [t for t in range(NT) if TILES[t][0] != 0]
OFF = {}
for half in (TA, TB):
    at = 0
    for t in half:
        OFF[t] = at
        at += ROWS[t]
COLS_A, COLS_B = sum(ROWS[t] for t in TA), sum(ROWS[t] for t in TB)


def runs(nodes):
    out = []
    for i, v in enumerate(nodes):
        if out and v == out[-1][1] + out[-1][2]:
            out[-1][2] += 1
        else:
            out.append([i, v, 1])
    return [tuple(r) for r in out]


class Window:

    def __init__(self, sg, l, slot, turn, out, enter=False, stats1=None, apply1=None, stats2=None, apply2=None):
        self.sg, self.l, self.slot, self.turn, self.out, self.enter = sg, l, slot, turn, out, enter
        self.stats1, self.apply1, self.stats2, self.apply2 = stats1, apply1, stats2, apply2
        self.feed = out == "step" or enter
        self.k = sg * STEPS + l * SLOTS + slot
        self.prev = (slot - 1) % SLOTS
        self.old = (slot - 2) % SLOTS
        self.visit = sg * SLOTS + slot - 2
        self.turned = sg * (STEPS - SLOTS) + l * SLOTS + slot - 2
        self.batch = (self.visit + SLOTS) * SB if enter else sg * CB + self.old * SB


def opening(sg, first=False):
    return Window(sg, 0, 0, None if first else "leave", None if first else "leave", enter=not first)


def supergroup(eng, sg, first=False, more=True):
    left, coming = (sg - 1) * SLOTS, (sg + 1) * SLOTS
    for slot in range(1, SLOTS):
        yield Window(sg, 0, slot, "step", "step" if slot >= 2 else None if first else "leave",
                     enter=slot == 1 and not first,
                     stats2=(left, 0) if slot == 2 and not first else None,
                     apply2=(left, 0) if slot == 3 and not first else None)
    with eng.Fori(1, LAYERS - 1) as l:
        for slot in range(SLOTS):
            yield Window(sg, l, slot, "step", "step",
                         stats1=coming + l - 1 if slot == 0 and more else None,
                         apply1=coming + l - 1 if slot == 1 and more else None,
                         stats2=(left + l, l) if slot == 2 and not first else None,
                         apply2=(left + l, l) if slot == 3 and not first else None)
    for slot in range(SLOTS):
        yield Window(sg, LAYERS - 1, slot, "leave" if slot else "step", "leave" if slot >= 2 else "step",
                     enter=more and slot >= 2,
                     stats1=coming + 3 if slot == 0 and more else None,
                     apply1=coming + 3 if slot == 1 and more else None,
                     stats2=None if more or slot < 3 else (sg * SLOTS, 0))


def windows(eng):
    yield opening(0, first=True)
    yield from supergroup(eng, 0, first=True)
    yield opening(1)
    with eng.Fori(1, CHUNKS - 1) as sg:
        yield from supergroup(eng, sg)
        yield opening(sg + 1)
    yield from supergroup(eng, CHUNKS - 1, more=False)
    yield None


def build(nc, x, adj, nodemask, W1, b1, W2, b2, fusion_w, weight, w_ih, w_hh, b_ih, b_hh, out):
    f32, f32r = mybir.dt.float32, mybir.dt.float32r
    ALU, ACT, AX = mybir.AluOpType, mybir.ActivationFunctionType, mybir.AxisListType
    ctx = ExitStack()
    with ctx:
        ctx.enter_context(nc.allow_non_contiguous_dma(reason="small rows of the adjacency"))

        def sb(name, shape, dt=f32):
            return ctx.enter_context(nc.sbuf_tensor(name, shape, dt))

        def sem(name):
            return ctx.enter_context(nc.semaphore(name))

        xn = sb("xn", [128, B, D])
        an = sb("an", [128, B, N])
        ident = sb("ident", [128, 128])
        w1 = sb("w1", [128, NG, HID])
        w2 = sb("w2", [128, NG, HC, D])
        rows = sb("rows", [NG * HC + NG + 6, 128])
        biasc = sb("biasc", [128, NG * HC + NG + 6])
        maskr = sb("maskr", [B, N])
        maskc = sb("maskc", [128, B])
        wh = sb("wh", [128, 2, GATES], f32r)
        wf = sb("wf", [128, LAYERS, 2, GATES], f32r)
        wcur = sb("wcur", [128, 2, GATES], f32r)
        gb = sb("gb", [128, 2])
        fw = sb("fw", [128, NG])
        fmx = sb("fmx", [128, 1])
        fsum = sb("fsum", [128, 1])
        fb2 = sb("fb2", [128, NG])
        ac = sb("ac", [128, CHUNKS, NT, FN])
        member = sb("member", [128, NT, FN])
        unit = sb("unit", [128, NT, FN])
        ksel = {k: sb(f"ksel{k}", [128, k]) for k in (4, 8, 16)}
        am = sb("am", [128, NT, FN])
        deg = sb("deg", [128, NT])
        zero = sb("zero", [128, NT])
        dinv = sb("dinv", [128, CHUNKS, NT])
        half = sb("half", [128, NT])
        tile_data = sb("tile_data", [128, 2 * NT * D])
        xt = tile_data[:, 0:NT * D].rearrange("p (t d) -> p t d", t=NT)
        s2 = tile_data[:, NT * D:].rearrange("p (t d) -> p t d", t=NT)
        bda = sb("bda", [128, COLS_A])
        bdb = sb("bdb", [128, COLS_B])
        na = sb("na", [128, COLS_A])
        nb = sb("nb", [128, COLS_B])
        ya = sb("ya", [128, COLS_A])
        yb = sb("yb", [128, COLS_B])
        ha = sb("ha", [128, HC, COLS_A])
        hb = sb("hb", [128, HC, COLS_B])
        fused = sb("fused", [128, CB * FN + 128])
        part = sb("part", [128, COLS_B])
        hT = sb("hT", [128, SLOTS, COLS])
        hhi = sb("hhi", [128, SLOTS, COLS], f32r)
        hlo = sb("hlo", [128, SLOTS, COLS], f32r)
        nat = sb("nat", [128, SLOTS, SB, D])
        ghi = sb("ghi", [128, SLOTS, COLS], f32r)
        glo = sb("glo", [128, SLOTS, COLS], f32r)
        rg = sb("rg", [128, 2, COLS])
        zg = sb("zg", [128, 2, COLS])
        cg = sb("cg", [128, 2, COLS])
        ng = sb("ng", [128, 2, COLS])
        dg = sb("dg", [128, 2, COLS])
        wir = rg[:, 0, 0:GATES].rearrange("p (c d) -> p c d", c=3)
        whr = rg[:, 1, 0:GATES].rearrange("p (c d) -> p c d", c=3)
        wl = zg[:].rearrange("p o (l d) -> p (o l) d", d=D)[:, 0:LAYERS, :]
        wlt = cg[:].rearrange("p o (l d) -> p (o l) d", d=D)[:, 0:LAYERS, :]
        wit = ng[:, 0, 0:GATES]
        yo = tile_data[:, 0:SLOTS * SB * D].rearrange("p (b d) -> p b d", d=D)
        st1, ag1, rs1, nm1 = sb("st1", [128, SB, 6]), sb("ag1", [128, SB, 2]), sb("rs1", [128, SB]), sb("nm1", [128, SB])
        st2, ag2, rs2, nm2 = sb("st2", [128, SB, 6]), sb("ag2", [128, SB, 2]), sb("rs2", [128, SB]), sb("nm2", [128, SB])

        P = [ctx.enter_context(nc.psum_tensor(f"p{i}", [128, 512], f32)) for i in range(8)]
        PR, PH, PZ, PI, PT, PX = P[:6]
        PG = P[6:8]

        def b1c(g, c):
            return biasc[:, g * HC + c:g * HC + c + 1]
        BI = NG * HC + NG
        bin_, bhn = biasc[:, BI + 2:BI + 3], biasc[:, BI + 5:BI + 6]

        w_in, wl_in, w1_in, w2_in, xt_in, xt_pool_in, xa_in = map(sem, (
            "w_in", "wl_in", "w1_in", "w2_in", "xt_in", "xt_pool_in", "xa_in"))
        ac0_in, ac1_in, ac_pool_in, ac_in = map(sem, ("ac0_in", "ac1_in", "ac_pool_in", "ac_in"))
        wlt_ok = sem("wlt_ok")
        ident_ok, ac_zero, dve_c, pool_c, exp_ok = map(sem, ("ident_ok", "ac_zero", "dve_c", "pool_c", "exp_ok"))
        prep_t, prep_a, prep_v, prep_f, prep_hi, prep_lo, fw_ok, b_ok = map(sem, (
            "prep_t", "prep_a", "prep_v", "prep_f", "prep_hi", "prep_lo", "fw_ok", "b_ok"))
        prep_c, deg_ok, pow_ok, am_ok, bd_ok = map(sem, ("prep_c", "deg_ok", "pow_ok", "am_ok", "bd_ok"))
        t_ps, y_ps, h_ps, s_ps, o_ps, f_ps = map(sem, ("t_ps", "y_ps", "h_ps", "s_ps", "o_ps", "f_ps"))
        na_ok, nb_ok, ya_ok, yb_ok, ha_ok, hb0_ok, hb1_ok, sa_ok, sb_ok, oa_ok, ob_ok, fused_ok, x_ok, a_ok = map(sem, (
            "na_ok", "nb_ok", "ya_ok", "yb_ok", "ha_ok", "hb0_ok", "hb1_ok", "sa_ok", "sb_ok", "oa_ok", "ob_ok", "fused_ok", "x_ok", "a_ok"))
        r_ps, i_ps, z_ps, T_ps, X_ps, F_ps, G_ps = map(sem, ("r_ps", "i_ps", "z_ps", "T_ps", "X_ps", "F_ps", "G_ps"))
        r_ok, z_ok, n_ok, t1_ok, c_ok, d_ok, e_ok, h_ok = map(sem, ("r_ok", "z_ok", "n_ok", "t1_ok", "c_ok", "d_ok", "e_ok", "h_ok"))
        hi_ok, lo_ok, nat_ok, ghi_ok, glo_ok, wcur_ok, hTx_ok = map(sem, (
            "hi_ok", "lo_ok", "nat_ok", "ghi_ok", "glo_ok", "wcur_ok", "hTx_ok"))
        bn1, ln1_st, ln1_rs, ln1_ok, x2_ok, sum_ok, bn2, ln2_st, ln2_rs, ln2_ok, out_ok = map(sem, (
            "bn1", "ln1_st", "ln1_rs", "ln1_ok", "x2_ok", "sum_ok", "bn2", "ln2_st", "ln2_rs", "ln2_ok", "out_ok"))
        yo_free, gathered, dev1, dev2 = map(sem, ("yo_free", "gathered", "dev1", "dev2"))
        waited = sem("waited")

        block = ctx.enter_context(nc.Block())

        def tile_rows(dram, c, t):
            g, k, b0 = TILES[t]
            for i, v, n in runs(GROUPS[g]):
                yield i * k, n * k, dram[bass.ds(c * CB + b0, k), v:v + n, :].rearrange("k n d -> n k d")

        def load_adj_rows(eng, c, done, tiles=range(NT)):
            for t in tiles:
                for r0, n, src in tile_rows(adj, c, t):
                    eng.dma_start(ac[r0:r0 + n, bass.ds(c, 1), t, :].rearrange("p o m -> p (o m)"),
                                  src[:, :, 0:FN]).then_inc(done, 16)

        def load_x_rows(eng, c, tiles, done):
            for t in tiles:
                for r0, n, src in tile_rows(x, c, t):
                    eng.dma_start(xt[r0:r0 + n, t, :], src).then_inc(done, 16)

        def load_chunk(eng, c):
            for dst, src in ((xn, x), (an, adj)):
                for b in (0, CB // 2):
                    eng.dma_start(dst[:, bass.ds(c * CB + b, CB // 2), :],
                                  src[bass.ds(c * CB + b, CB // 2), :, :].rearrange("b n d -> n b d")).then_inc(xa_in, 16)

        def group_cols(g):
            mine = [t for t in TB if TILES[t][0] == g]
            return OFF[mine[0]], OFF[mine[-1]] + ROWS[mine[-1]]

        F_BANKS, F_BANKS_LAST = (2, 5, 3, 4), (4, 3, 2, 1)
        ADDS = sum(len(runs(GROUPS[TILES[t][0]])) for t in TB)

        def n_runs(tiles):
            return sum(len(runs(GROUPS[TILES[t][0]])) for t in tiles)
        N_RUNS = n_runs(range(NT))
        XT_SP, XT_POOL = range(0, NT - 2), range(NT - 2, NT)

        def wait_alone(eng, signal, value):
            eng.wait_ge(signal, value)
            eng.sem_inc(waited, 1)

        @block.sync
        def _(sp):
            sp.wait_ge(ac_zero, 1)
            load_adj_rows(sp, 0, ac0_in)
            for i, (name, src) in enumerate((("b1", b1.rearrange("g (c h) -> (g c) h", c=HC)), ("b2", b2),
                                             ("b_ih", b_ih.rearrange("(c h) -> c h", h=128)),
                                             ("b_hh", b_hh.rearrange("(c h) -> c h", h=128)))):
                r0 = (0, NG * HC, NG * HC + NG, NG * HC + NG + 3)[i]
                sp.dma_start(rows[r0:r0 + src.shape[0], :], src).then_inc(w_in, 16)
            sp.dma_start(maskr[:], nodemask).then_inc(w_in, 16)
            sp.dma_start(fw[:], fusion_w.partition_broadcast(128)).then_inc(w_in, 16)
            sp.dma_start(w1[:], W1.rearrange("g d h -> d g h")).then_inc(w1_in, 16)
            load_x_rows(sp, 0, XT_SP, xt_in)
            sp.dma_start(w2[:], W2.rearrange("g (c h) d -> h g c d", c=HC)).then_inc(w2_in, 16)
            sp.wait_ge(ac_zero, 2)
            load_adj_rows(sp, 1, ac1_in, TB)
            load_chunk(sp, 0)

            def load_x(c):
                sp.wait_ge(y_ps, 2 * c - 1)
                load_x_rows(sp, c, TA, xt_in)
                sp.wait_ge(y_ps, 2 * c)
                load_x_rows(sp, c, [t for t in XT_SP if t not in TA], xt_in)

            with sp.Fori(1, CHUNKS - 1) as c:
                load_x(c)
                load_adj_rows(sp, c + 1, ac_in, TB)
                sp.wait_ge(xa_in, 64 * c)
                load_chunk(sp, c)
                wait_alone(sp, ac_in, 16 * n_runs(TB) * c)
            load_x(CHUNKS - 1)
            sp.wait_ge(xa_in, 64 * (CHUNKS - 1))
            load_chunk(sp, CHUNKS - 1)
            sp.sem_inc(yo_free, SLOTS)
            with sp.Fori(0, CHUNKS) as sg:
                for slot in range(SLOTS):
                    v = sg * SLOTS + slot
                    sp.wait_ge(ln2_ok, v + 1)
                    sp.dma_start(out[bass.ds(v * SB, SB), :, :].rearrange("b n d -> n b d"),
                                 yo[:, slot * SB:(slot + 1) * SB, :]).then_inc(out_ok, 16)
                    sp.wait_ge(out_ok, 16 * (v + 1))
                    sp.sem_inc(yo_free, 1)
            sp.wait_ge(out_ok, 16 * (B // SB))

        def counter(eng, signal):
            n = [0]

            def link(ins):
                n[0] += 1
                ins.then_inc(signal, 1)
                eng.wait_ge(signal, n[0])
            return link

        @block.gpsimd
        def _(pool):
            link = counter(pool, pool_c)
            nc.gpsimd.memset(ac[:, 0], 0.0).then_inc(ac_zero, 1)
            link(nc.gpsimd.memset(ident[:], 0.0))
            nc.gpsimd.affine_select(out=ident[:], in_=ident[:], compare_op=ALU.not_equal, fill=1.0, base=0,
                                    pattern=[[-1, 128]], channel_multiplier=1).then_inc(ident_ok, 1)
            nc.gpsimd.memset(fused[:], 0.0)
            nc.gpsimd.memset(ac[:, 1:], 0.0).then_inc(ac_zero, 1)
            link(nc.gpsimd.memset(half[:], -0.5))
            load_x_rows(pool, 0, XT_POOL, xt_pool_in)

            def load_adj(c):
                if c > 1:
                    pool.wait_ge(ac_pool_in, 16 * n_runs(TA) * (c - 1))
                load_adj_rows(pool, c, ac_pool_in, TA)

            load_adj(1)

            def power(c):
                wait_alone(pool, deg_ok, c + 1)
                nc.gpsimd.tensor_tensor(dinv[:, bass.ds(c, 1), :].rearrange("p o t -> p (o t)"), deg[:], half[:],
                                        ALU.pow).then_inc(pow_ok, 1)

            def spread(c):
                wait_alone(pool, am_ok, c + 1)
                for t0, nt, pieces in ((0, 4, [(0, 0, 1, 25)]), (4, 2, [(0, 0, 1, 9)]), (6, 1, [(0, 0, 1, 1), (1, 9, 1, 6)]),
                                       (7, 1, [(0, 6, 2, 3)]), (8, 1, [(0, 3, 2, 3)])):
                    k, r, o = TILES[t0][1], ROWS[t0], OFF[t0]
                    dst = bda if t0 == 0 else bdb
                    a_t = am[0:r, t0:t0 + nt, :]
                    for i, v, s, n in pieces:
                        src = a_t[:, :, v:v + n] if s == 1 else a_t[:, 0, v:v + 12].rearrange("p (s m) -> p s m", s=2)[:, :, 0:n]
                        a = nt * s
                        d = dst[0:r, o + i * k:o + i * k + a * n * k].rearrange("p (a m k) -> p a m k", a=a, k=k)
                        last = nc.gpsimd.tensor_tensor(
                            d, src.unsqueeze(3).to_broadcast([r, a, n, k]),
                            ksel[k][0:r, :].unsqueeze(1).unsqueeze(1).to_broadcast([r, a, n, k]), ALU.mult)
                last.then_inc(bd_ok, 1)

            def deviation(ag, rs, nm, done, visit):
                nc.gpsimd.tensor_scalar(rs, ag[:, :, 1], EPS, 1.0, ALU.add, ALU.mult).then_inc(done, 1)
                nc.gpsimd.tensor_scalar(nm, ag[:, :, 0], -1.0, 0.0, ALU.mult, ALU.add).then_inc(done, 1)
                pool.wait_ge(done, 3 * visit + 1)
                nc.gpsimd.tensor_tensor(rs, rs, half[:, 0:SB], ALU.pow).then_inc(done, 1)
                pool.wait_ge(done, 3 * visit + 3)
                return nc.gpsimd.tensor_tensor(nm, nm, rs, ALU.mult)

            def deviation1(visit):
                wait_alone(pool, ln1_st, visit + 1)
                deviation(ag1, rs1[:], nm1[:], dev1, visit).then_inc(ln1_rs, 1)

            def deviation2(visit):
                wait_alone(pool, ln2_st, visit + 1)
                deviation(ag2, rs2[:], nm2[:], dev2, visit).then_inc(ln2_rs, 1)

            def prepare(c):
                pool.wait_ge(y_ps, 2 * c)
                load_x_rows(pool, c, XT_POOL[1:], xt_pool_in)
                power(c)
                load_x_rows(pool, c, XT_POOL[:1], xt_pool_in)
                pool.wait_ge(t_ps, 2 * c)
                spread(c)

            power(0)
            spread(0)
            load_adj(2)
            prepare(1)
            load_adj(3)
            with pool.Fori(0, CHUNKS - 2) as c:
                prepare(c + 2)
                deviation1(c)
                wait_alone(pool, ln1_ok, c + 1)
            deviation1(2)
            pool.wait_ge(ln1_ok, 3)
            deviation1(3)
            for w in windows(pool):
                if w:
                    pool.wait_ge(n_ok, w.k + 1)
                    nc.gpsimd.tensor_tensor(dg[:, w.slot % 2, :], hT[:, w.slot, :], ng[:, w.slot % 2, :],
                                            ALU.subtract).then_inc(d_ok, 1)
                    if w.stats1 is not None:
                        deviation1(w.stats1)
                    if w.stats2:
                        deviation2(w.stats2[0])
                else:
                    for slot in range(1, SLOTS):
                        deviation2((CHUNKS - 1) * SLOTS + slot)

        @block.scalar
        def _(act):
            act.dma_start(wir, w_ih.rearrange("(c e) d -> e c d", c=3)).then_inc(wl_in, 16)
            act.dma_start(whr, w_hh.rearrange("(c e) d -> e c d", c=3)).then_inc(wl_in, 16)
            act.dma_start(wl, weight.rearrange("l c e -> c l e")).then_inc(wl_in, 16)
            act.wait_ge(prep_t, 1)
            nc.scalar.copy(wit, P[0][:, 0:GATES])
            act.wait_ge(prep_t, 2)
            nc.scalar.copy(wh[:, 0, :], P[1][:, 0:GATES]).then_inc(prep_hi, 1)
            act.wait_ge(prep_t, 3)
            nc.scalar.copy(wlt[:, 0:4, :], P[2][:].rearrange("p (l d) -> p l d", l=4))
            act.wait_ge(prep_t, 4)
            nc.scalar.copy(wlt[:, 4, :], P[3][:, 0:128]).then_inc(wlt_ok, 1)
            for l in range(LAYERS):
                act.wait_ge(prep_f, l + 1)
                nc.scalar.copy(wf[:, l, 0, :], P[(4 + l) % 8][:, 0:GATES]).then_inc(prep_hi, 1)
            act.wait_ge(fw_ok, 1)
            nc.scalar.activation(fw[:], fw[:], ACT.Exp, bias=fmx[:], accum_out=fsum[:]).then_inc(exp_ok, 1)
            act.wait_ge(prep_t, 5)
            nc.scalar.copy(maskc[:], P[3][:, 256:256 + B])
            nc.scalar.copy(biasc[:], P[3][:, 128:128 + NG * HC + NG + 6]).then_inc(prep_a, 1)
            act.wait_ge(b_ok, 1)
            def adjacency(c):
                act.wait_ge(t_ps, 2 * c + 1)
                for t in TA:
                    r, o = ROWS[t], OFF[t]
                    dv = dinv[0:r, bass.ds(c, 1), t:t + 1].rearrange("p o t -> p (o t)")
                    last = nc.scalar.activation(na[0:r, o:o + r], P[2][0:r, o:o + r], ACT.Identity, scale=dv)
                last.then_inc(na_ok, 1)

            def neighbours(c):
                act.wait_ge(y_ps, 2 * c + 1)
                nc.scalar.copy(ya[:], P[2][:, 0:COLS_A]).then_inc(ya_ok, 1)

            def hidden(c):
                for h in range(HC):
                    act.wait_ge(h_ps, 4 * c + 1 + h)
                    nc.scalar.activation(ha[:, h, :], P[6 + h][:, 0:COLS_A], ACT.Relu, bias=b1c(0, h)).then_inc(ha_ok, 1)
                act.wait_ge(h_ps, 4 * c + 4)
                for g in range(1, NG):
                    a, b = group_cols(g)
                    last = nc.scalar.activation(hb[:, 1, a:b], P[1][:, a:b], ACT.Relu, bias=b1c(g, 1))
                last.then_inc(hb1_ok, 1)
                act.wait_ge(s_ps, 3 * c + 1)
                nc.scalar.copy(s2[0:ROWS[0], 0:4, :], P[6][0:ROWS[0], :].rearrange("p (t d) -> p t d", t=4)).then_inc(sa_ok, 1)

            def output_a(c):
                act.wait_ge(o_ps, 2 * c + 1)
                nc.scalar.activation(fused[:, 0:CB * FN].rearrange("p (t k n) -> p t n k", t=4, n=FN),
                                     P[3][:, 0:COLS_A].rearrange("p (t n k) -> p t n k", t=4, n=FN),
                                     ACT.Relu, bias=fb2[:, 0:1], scale=fw[:, 0:1]).then_inc(oa_ok, 1)

            def output_b(c):
                act.wait_ge(o_ps, 2 * c + 2)
                for g in range(1, NG):
                    a, b = group_cols(g)
                    last = nc.scalar.activation(part[:, a:b], P[4][:, a:b], ACT.Relu, bias=fb2[:, g:g + 1], scale=fw[:, g:g + 1])
                last.then_inc(ob_ok, 1)

            def norm1(visit, part=range(SB)):
                if 0 in part:
                    act.wait_ge(ln1_rs, visit + 1)
                for q in part:
                    xq = xn[:, bass.ds(visit * SB + q, 1), :].rearrange("p o d -> p (o d)")
                    last = nc.scalar.activation(xq, xq, ACT.Identity, bias=nm1[:, q:q + 1], scale=rs1[:, q:q + 1])
                if SB - 1 in part:
                    last.then_inc(ln1_ok, 1)

            def norm2(visit, slot, part=range(SB)):
                if 0 in part:
                    act.wait_ge(ln2_rs, visit + 1)
                for q in part:
                    yq = yo[:, bass.ds(slot * SB + q, 1), :].rearrange("p o d -> p (o d)")
                    last = nc.scalar.activation(yq, yq, ACT.Identity, bias=nm2[:, q:q + 1], scale=rs2[:, q:q + 1])
                if SB - 1 in part:
                    last.then_inc(ln2_ok, 1)

            def apply(w, part):
                if w.apply1 is not None:
                    norm1(w.apply1, part)
                if w.apply2:
                    norm2(*w.apply2, part)

            def turn_over(c):
                act.wait_ge(o_ps, 2 * c + 1)
                adjacency(c + 1)
                output_a(c)

            adjacency(0)
            neighbours(0)
            hidden(0)
            turn_over(0)
            with act.Fori(0, CHUNKS - 2) as c:
                neighbours(c + 1)
                output_b(c)
                hidden(c + 1)
                turn_over(c + 1)
                norm1(c)
            neighbours(CHUNKS - 1)
            output_b(CHUNKS - 2)
            hidden(CHUNKS - 1)
            output_a(CHUNKS - 1)
            output_b(CHUNKS - 1)
            def aggregated(m, s, par):
                act.wait_ge(G_ps, m + 1)
                nc.scalar.copy(ghi[:, s, :], PG[par][:]).then_inc(ghi_ok, 1)

            for s in range(SLOTS):
                act.wait_ge(X_ps, s + 1)
                nc.scalar.copy(hT[:, s, :], PX[:])
                nc.scalar.copy(hhi[:, s, :], PX[:]).then_inc(hi_ok, 1)
                if s < 2:
                    norm1(s + 2)
                aggregated(s, s, s % 2)
            for w in windows(act):
                if w:
                    k, s, p = w.k, w.slot, w.slot % 2
                    if w.enter:
                        act.wait_ge(G_ps, k - 1)
                        wait_alone(act, ln1_ok, w.visit + SLOTS + 1)
                        nc.scalar.activation(nat[:, w.old], xn[:, bass.ds(w.batch, SB), :], ACT.Identity).then_inc(x2_ok, 1)
                    if w.out == "step":
                        act.wait_ge(T_ps, w.turned + 1)
                        nc.scalar.copy(nat[:, w.old], PT[:].rearrange("p (b d) -> p b d", b=SB)).then_inc(nat_ok, 1)
                    act.wait_ge(r_ps, k + 1)
                    nc.scalar.activation(rg[:, p, :], PR[:], ACT.Sigmoid, bias=gb[:, 0:1]).then_inc(r_ok, 1)
                    apply(w, range(2))
                    if w.enter:
                        act.wait_ge(X_ps, w.visit + SLOTS + 1)
                        nc.scalar.copy(hT[:, w.old, :], PX[:])
                        nc.scalar.copy(hhi[:, w.old, :], PX[:]).then_inc(hi_ok, 1)
                    act.wait_ge(z_ps, k + 1)
                    nc.scalar.activation(zg[:, p, :], PZ[:], ACT.Sigmoid, bias=gb[:, 1:2]).then_inc(z_ok, 1)
                    act.wait_ge(c_ok, k + 1)
                    nc.scalar.activation(ng[:, p, :], cg[:, p, :], ACT.Tanh, bias=bin_).then_inc(n_ok, 1)
                    if w.feed:
                        aggregated(k + 2, w.old, s % 2)
                    if w.turn == "step":
                        act.wait_ge(h_ok, k)
                        nc.scalar.copy(hhi[:, w.prev, :], hT[:, w.prev, :]).then_inc(hi_ok, 1)
                    apply(w, range(2, SB))
                else:
                    for slot in range(SLOTS):
                        norm2((CHUNKS - 1) * SLOTS + slot, slot)

        @block.vector
        def _(dve):
            link = counter(dve, dve_c)
            TT, TS, STT = nc.vector.tensor_tensor, nc.vector.tensor_scalar, nc.vector.scalar_tensor_tensor
            link(nc.vector.memset(member[:], 0.0))
            link(nc.vector.memset(unit[:], 0.0))
            dve.wait_ge(ident_ok, 1)
            for t, (g, k, _) in enumerate(TILES):
                for i, v, n in runs(GROUPS[g]):
                    nc.vector.memset(member[:, t, v:v + n], 1.0)
                    nc.vector.reduce_sum(unit[:, t, v:v + n],
                                         ident[:, i * k:(i + n) * k].rearrange("p (n k) -> p n k", k=k), AX.X)
            for k in ksel:
                last = nc.vector.reduce_sum(ksel[k][:], ident[:].rearrange("p (n k) -> p k n", k=k), AX.X)
            link(last)
            def degrees(c):
                if not isinstance(c, int) or c:
                    dve.wait_ge(bd_ok, c)
                if isinstance(c, int):
                    if c:
                        dve.wait_ge(ac_pool_in, 16 * n_runs(TA))
                    wait_alone(dve, (ac0_in, ac1_in)[c], 16 * n_runs(TB if c else range(NT)))
                else:
                    wait_alone(dve, ac_pool_in, 16 * n_runs(TA) * c)
                    wait_alone(dve, ac_in, 16 * n_runs(TB) * (c - 1))
                flat = am[:].rearrange("p t m -> p (t m)")
                TT(flat, ac[:, bass.ds(c, 1)].rearrange("p o t m -> p (o t m)"), member[:].rearrange("p t m -> p (t m)"),
                   ALU.mult).then_inc(prep_c, 1)
                dve.wait_ge(prep_c, 6 * c + 1)
                TT(flat, flat, unit[:].rearrange("p t m -> p (t m)"), ALU.add).then_inc(prep_c, 1)
                wait_alone(dve, prep_c, 6 * c + 2)
                nc.vector.reduce_sum(deg[:], am[:], AX.X).then_inc(prep_c, 1)
                wait_alone(dve, prep_c, 6 * c + 3)
                TS(zero[:], deg[:], 0.0, None, ALU.is_equal).then_inc(prep_c, 1)
                dve.wait_ge(prep_c, 6 * c + 4)
                TT(deg[:], deg[:], zero[:], ALU.add).then_inc(deg_ok, 1)
                TS(zero[:], zero[:], -1.0, 1.0, ALU.mult, ALU.add).then_inc(prep_c, 1)

            def scaled(c):
                dve.wait_ge(pow_ok, c + 1)
                wait_alone(dve, prep_c, 6 * c + 5)
                dv = dinv[:, bass.ds(c, 1), :].rearrange("p o t -> p (o t)")
                TT(dv, dv, zero[:], ALU.mult).then_inc(prep_c, 1)
                dve.wait_ge(prep_c, 6 * c + 6)
                TT(am[:], am[:], dv.unsqueeze(2).to_broadcast([128, NT, FN]), ALU.mult).then_inc(am_ok, 1)

            degrees(0)
            dve.wait_ge(prep_hi, 1)
            TT(wh[:, 1, :], P[1][:, 0:GATES], wh[:, 0, :], ALU.subtract)
            scaled(0)
            for l in range(LAYERS):
                dve.wait_ge(prep_hi, l + 2)
                TT(wf[:, l, 1, :], P[(4 + l) % 8][:, 0:GATES], wf[:, l, 0, :], ALU.subtract).then_inc(prep_lo, 1)
            dve.wait_ge(w_in, 16 * 6)
            nc.vector.tensor_reduce(fmx[:], fw[:], AX.X, ALU.max, negate=True).then_inc(fw_ok, 1)
            dve.wait_ge(exp_ok, 1)
            link(nc.vector.reciprocal(fsum[:], fsum[:]))
            link(TS(fw[:], fw[:], fsum[:], None, ALU.mult))
            dve.wait_ge(prep_a, 1)
            TT(gb[:], biasc[:, BI:BI + 2], biasc[:, BI + 3:BI + 5], ALU.add)
            TT(fb2[:], biasc[:, NG * HC:BI], fw[:], ALU.mult).then_inc(b_ok, 1)
            def adjacency(c):
                dve.wait_ge(t_ps, 2 * c + 2)
                for t in TB:
                    r, o = ROWS[t], OFF[t]
                    dv = dinv[0:r, bass.ds(c, 1), t:t + 1].rearrange("p o t -> p (o t)")
                    last = TS(nb[0:r, o:o + r], P[5][0:r, o:o + r], dv, None, ALU.mult)
                last.then_inc(nb_ok, 1)

            def neighbours(c):
                dve.wait_ge(y_ps, 2 * c + 2)
                nc.vector.tensor_copy(yb[:], P[5][:, 0:COLS_B]).then_inc(yb_ok, 1)

            def hidden(c):
                dve.wait_ge(h_ps, 4 * c + 3)
                for g in range(1, NG):
                    a, b = group_cols(g)
                    last = TS(hb[:, 0, a:b], P[0][:, a:b], b1c(g, 0), 0.0, ALU.add, ALU.max)
                last.then_inc(hb0_ok, 1)

            def second(c):
                dve.wait_ge(s_ps, 3 * c + 2)
                nc.vector.tensor_copy(s2[0:ROWS[4], 4:6, :], P[7][0:ROWS[4], 0:256].rearrange("p (t d) -> p t d", t=2))
                dve.wait_ge(s_ps, 3 * c + 3)
                nc.vector.tensor_copy(s2[0:ROWS[6], 6, :], P[0][0:ROWS[6], 0:128])
                nc.vector.tensor_copy(s2[0:ROWS[7], 7:9, :], P[0][0:ROWS[7], 128:384].rearrange("p (t d) -> p t d", t=2)).then_inc(sb_ok, 1)

            def gather(c):
                dve.wait_ge(oa_ok, c + 1)
                wait_alone(dve, ob_ok, c + 1)
                f = fused[:, 0:CB * FN].rearrange("p (b n) -> p b n", n=FN)
                n_add = 0
                for t in TB:
                    g, k, b0 = TILES[t]
                    for i, v, n in runs(GROUPS[g]):
                        d = f[:, b0:b0 + k, v:v + n]
                        s = part[:, OFF[t] + i * k:OFF[t] + (i + n) * k].rearrange("p (n k) -> p k n", k=k)
                        if n_add:
                            dve.wait_ge(gathered, ADDS * c + n_add)
                        n_add += 1
                        TT(d, d, s, ALU.add).then_inc(gathered, 1)

            def add(c, banks):
                dve.wait_ge(xa_in, 64 * c + 64)
                for q in range(4):
                    wait_alone(dve, f_ps, 4 * c + q + 1)
                    xq = xn[0:FN, bass.ds(c * CB + q * 4, 4), :]
                    TT(xq, xq, P[banks[q]][0:FN, :].rearrange("p (b d) -> p b d", b=4), ALU.add).then_inc(x_ok, 1)

            def ones(c):
                dve.wait_ge(xa_in, 64 * c + 64)
                ab = an[:, bass.ds(c * CB, CB), :]
                TS(ab, ab, 0.0, None, ALU.not_equal).then_inc(a_ok, 1)

            def norm1(visit, b):
                for q in range(SB):
                    last = nc.vector.bn_stats(st1[:, q, :], xn[:, bass.ds(b + q, 1), :].rearrange("p o d -> p (o d)"))
                last.then_inc(bn1, 1)
                wait_alone(dve, bn1, visit + 1)
                for q in range(SB):
                    last = nc.vector.bn_aggr(ag1[:, q, :], st1[:, q, :])
                last.then_inc(ln1_st, 1)

            def settle(s, b, ready):
                wait_alone(dve, ln1_ok, ready)
                nc.vector.tensor_copy(nat[:, s], xn[:, bass.ds(b, SB), :]).then_inc(x2_ok, 1)

            adjacency(0)
            neighbours(0)
            degrees(1)
            hidden(0)
            scaled(1)
            second(0)

            def chunk(c, more):
                dve.wait_ge(o_ps, 2 * c + 2)
                adjacency(c + 1)
                if more:
                    degrees(c + 2)
                neighbours(c + 1)
                gather(c)
                hidden(c + 1)
                if more:
                    scaled(c + 2)
                add(c, F_BANKS)
                wait_alone(dve, x_ok, 4)
                norm1(c, c * SB)
                second(c + 1)
                if more:
                    ones(c)
                wait_alone(dve, ln1_rs, c + 1)

            with dve.Fori(0, CHUNKS - 2) as c:
                chunk(c, True)
            chunk(CHUNKS - 2, False)
            def end_step(k, s):
                dve.wait_ge(d_ok, k)
                TT(dg[:, s % 2, :], zg[:, s % 2, :], dg[:, s % 2, :], ALU.mult).then_inc(e_ok, 1)
                dve.wait_ge(e_ok, k)
                TT(hT[:, s, :], ng[:, s % 2, :], dg[:, s % 2, :], ALU.add).then_inc(h_ok, 1)

            def lo_state(m, s):
                dve.wait_ge(hi_ok, m + 1)
                TT(hlo[:, s, :], hT[:, s, :], hhi[:, s, :], ALU.subtract).then_inc(lo_ok, 1)

            def lo_neighbours(m, s, par):
                dve.wait_ge(ghi_ok, m + 1)
                TT(glo[:, s, :], PG[par][:], ghi[:, s, :], ALU.subtract).then_inc(glo_ok, 1)

            def leave(visit, slot, bank):
                dve.wait_ge(F_ps, visit + 1)
                dve.wait_ge(yo_free, visit + 1)
                for q in range(SB):
                    b = visit * SB + q
                    last = STT(yo[:, slot * SB + q, :], bank[:, q * D:(q + 1) * D], maskc[:, bass.ds(b, 1)],
                               xn[:, bass.ds(b, 1), :].rearrange("p o d -> p (o d)"), ALU.mult, ALU.add)
                last.then_inc(sum_ok, 1)

            def norm2(visit, slot):
                if isinstance(visit, int):
                    if visit:
                        wait_alone(dve, ln2_st, visit)
                else:
                    wait_alone(dve, yo_free, visit + SLOTS)
                dve.wait_ge(sum_ok, visit + 1)
                for q in range(SB):
                    last = nc.vector.bn_stats(st2[:, q, :], yo[:, bass.ds(slot * SB + q, 1), :].rearrange("p o d -> p (o d)"))
                last.then_inc(bn2, 1)
                wait_alone(dve, bn2, visit + 1)
                if isinstance(visit, int) and visit:
                    wait_alone(dve, ln2_ok, visit)
                for q in range(SB):
                    last = nc.vector.bn_aggr(ag2[:, q, :], st2[:, q, :])
                last.then_inc(ln2_st, 1)

            def layer_weights(l):
                nc.vector.tensor_copy(wcur[:], wf[:, bass.ds(l, 1)].rearrange("p o h e -> p (o h) e")).then_inc(wcur_ok, 1)

            settle(0, 0, 1)
            settle(1, SB, 2)
            norm1(SLOTS - 1, (SLOTS - 1) * SB)
            gather(CHUNKS - 1)
            for s in range(2):
                settle(s + 2, (s + 2) * SB, s + 3)
                lo_state(s, s)
                lo_neighbours(s, s, s % 2)
            add(CHUNKS - 1, F_BANKS_LAST)
            layer_weights(0)
            for s in range(2, SLOTS):
                lo_state(s, s)
                lo_neighbours(s, s, s % 2)
            ones(CHUNKS - 2)
            ones(CHUNKS - 1)
            for w in windows(dve):
                if w:
                    k, s, p = w.k, w.slot, w.slot % 2
                    if w.out == "leave":
                        leave(w.visit, w.old, PT)
                    dve.wait_ge(r_ok, k + 1)
                    STT(cg[:, p, :], PH[:], bhn, rg[:, p, :], ALU.add, ALU.mult).then_inc(t1_ok, 1)
                    dve.wait_ge(i_ps, k + 1)
                    dve.wait_ge(t1_ok, k + 1)
                    TT(cg[:, p, :], cg[:, p, :], PI[:], ALU.add).then_inc(c_ok, 1)
                    if w.turn:
                        end_step(k, w.prev)
                    if w.stats1 is not None:
                        dve.wait_ge(ln1_ok, w.stats1)
                        norm1(w.stats1, w.stats1 * SB)
                    if w.stats2:
                        norm2(*w.stats2)
                    if w.enter:
                        lo_state(k + 2, w.old)
                    last_layer = isinstance(w.l, int) and w.l == LAYERS - 1
                    if s == SLOTS - 1 and not (last_layer and not w.enter):
                        wait_alone(dve, z_ps, k + 1)
                        layer_weights(0 if last_layer else w.l + 1)
                    if w.feed:
                        lo_neighbours(k + 2, w.old, s % 2)
                    if w.turn == "step":
                        lo_state(k + 3, w.prev)
                else:
                    last = B // SB - 1
                    leave(last - 1, SLOTS - 2, PT)
                    norm2(last - 2, SLOTS - 3)
                    end_step(B // SB * LAYERS, SLOTS - 1)
                    norm2(last - 1, SLOTS - 2)
                    leave(last, SLOTS - 1, PX)
                    norm2(last, SLOTS - 1)

        @block.tensor
        def _(pe):
            MM, TR = nc.tensor.matmul, nc.tensor.transpose
            pe.wait_ge(ident_ok, 1)
            pe.wait_ge(wl_in, 48)
            for i in range(3):
                last = TR(P[0][:, i * 128:(i + 1) * 128], wir[:, i, :], ident[:])
            last.then_inc(prep_t, 1)
            for i in range(3):
                last = TR(P[1][:, i * 128:(i + 1) * 128], whr[:, i, :], ident[:])
            last.then_inc(prep_t, 1)
            for l in range(4):
                last = TR(P[2][:, l * 128:(l + 1) * 128], wl[:, l, :], ident[:])
            last.then_inc(prep_t, 1)
            TR(P[3][:, 0:128], wl[:, 4, :], ident[:]).then_inc(prep_t, 1)
            pe.wait_ge(wlt_ok, 1)
            for l in range(LAYERS):
                MM(P[(4 + l) % 8][:, 0:GATES], wlt[:, l, :], wit, start=True, stop=True).then_inc(prep_f, 1)
            pe.wait_ge(w_in, 16 * 6)
            nr = NG * HC + NG + 6
            TR(P[3][:, 128:128 + nr], rows[:], ident[0:nr, 0:nr])
            TR(P[3][:, 256:256 + B], maskr[:], ident[0:B, 0:B]).then_inc(prep_t, 1)
            pe.wait_ge(prep_lo, LAYERS)

            def adjacency(c):
                pe.wait_ge(bd_ok, c + 1)
                for half, bd, bank in ((TA, bda, 2), (TB, bdb, 5)):
                    for t in half:
                        r, o = ROWS[t], OFF[t]
                        last = TR(P[bank][0:r, o:o + r], bd[0:r, o:o + r], ident[0:r, 0:r])
                    last.then_inc(t_ps, 1)

            def first(c):
                pe.wait_ge(xt_in, 16 * n_runs(XT_SP) * (c + 1))
                pe.wait_ge(xt_pool_in, 16 * n_runs(XT_POOL) * (c + 1))
                for half, nn, bank, ready in ((TA, na, 2, na_ok), (TB, nb, 5, nb_ok)):
                    pe.wait_ge(ready, c + 1)
                    for t in half:
                        r, o = ROWS[t], OFF[t]
                        last = MM(P[bank][:, o:o + r], xt[0:r, t, :], nn[0:r, o:o + r], start=True, stop=True)
                    last.then_inc(y_ps, 1)
                if isinstance(c, int):
                    pe.wait_ge(w1_in, 16)
                pe.wait_ge(ya_ok, c + 1)
                for h in range(HC):
                    MM(P[6 + h][:, 0:COLS_A], w1[:, 0, h * 128:(h + 1) * 128], ya[:], start=True, stop=True).then_inc(h_ps, 1)
                pe.wait_ge(yb_ok, c + 1)
                for h in range(HC):
                    for g in range(1, NG):
                        a, b = group_cols(g)
                        last = MM(P[h][:, a:b], w1[:, g, h * 128:(h + 1) * 128], yb[:, a:b], start=True, stop=True)
                    last.then_inc(h_ps, 1)

            def times_w2(tiles, hid, bank):
                for i, t in enumerate(tiles):
                    g, r, o = TILES[t][0], ROWS[t], OFF[t]
                    for h in range(HC):
                        last = MM(P[bank][0:r, i * D:(i + 1) * D], hid[:, h, o:o + r], w2[:, g, h, :],
                                  start=(h == 0), stop=(h == HC - 1))
                last.then_inc(s_ps, 1)

            def second(c):
                pe.wait_ge(ha_ok, 2 * c + 2)
                times_w2(TA, ha, 6)
                pe.wait_ge(hb0_ok, c + 1)
                pe.wait_ge(hb1_ok, c + 1)
                times_w2(TB[0:2], hb, 7)
                times_w2(TB[2:5], hb, 0)

            def output(c):
                for half, nn, bank, ready in ((TA, na, 3, sa_ok), (TB, nb, 4, sb_ok)):
                    pe.wait_ge(ready, c + 1)
                    for t in half:
                        r, o = ROWS[t], OFF[t]
                        last = MM(P[bank][:, o:o + r], s2[0:r, t, :], nn[0:r, o:o + r], start=True, stop=True)
                    last.then_inc(o_ps, 1)

            def back(c, banks):
                pe.wait_ge(gathered, ADDS * (c + 1))
                for q in range(4):
                    for i in range(4):
                        b = 4 * q + i
                        last = TR(P[banks[q]][:, i * D:(i + 1) * D], fused[:, b * FN:b * FN + 128], ident[:])
                    last.then_inc(f_ps, 1)

            adjacency(0)
            first(0)
            pe.wait_ge(w2_in, 16)
            second(0)
            with pe.Fori(0, CHUNKS - 1) as c:
                adjacency(c + 1)
                output(c)
                first(c + 1)
                back(c, F_BANKS)
                second(c + 1)
                pe.wait_ge(x_ok, 4 * c + 4)
            output(CHUNKS - 1)
            def turn(bank, src):
                for q in range(SB):
                    last = TR(bank[:, q * 128:(q + 1) * 128], src(q), ident[:])
                return last

            def aggregate(s, b, par):
                for q in range(SB):
                    last = MM(PG[par][:, q * N:(q + 1) * N], nat[:, s, q, :],
                              an[:, bass.ds(b + q, 1), :].rearrange("p o n -> p (o n)"), start=True, stop=True)
                last.then_inc(G_ps, 1)

            def product(bank, w, g, xhi, xlo, start, stop):
                cols = slice(g * D, (g + 1) * D)
                MM(bank[:], w[:, 0, cols], xhi, start=start, stop=False)
                MM(bank[:], w[:, 0, cols], xlo, start=False, stop=False)
                return MM(bank[:], w[:, 1, cols], xhi, start=False, stop=stop)

            def enter(s):
                pe.wait_ge(x2_ok, s + 1)
                if s:
                    pe.wait_ge(hi_ok, s)
                turn(PX, lambda q: nat[:, s, q, :]).then_inc(X_ps, 1)
                if s >= 2:
                    pe.wait_ge(glo_ok, s - 1)
                aggregate(s, s * SB, s % 2)

            pe.wait_ge(a_ok, 1)
            enter(0)
            enter(1)
            back(CHUNKS - 1, F_BANKS_LAST)
            enter(2)
            enter(3)
            pe.wait_ge(x_ok, 4 * CHUNKS)
            for w in windows(pe):
                if w:
                    k, s = w.k, w.slot
                    xhi, xlo = hhi[:, s, :], hlo[:, s, :]
                    pe.wait_ge(hi_ok, k + 1)
                    pe.wait_ge(lo_ok, k + 1)
                    if w.turn:
                        pe.wait_ge(r_ok, k)
                    product(PR, wh, 0, xhi, xlo, True, False)
                    if w.turn:
                        pe.wait_ge(t1_ok, k)
                    product(PH, wh, 2, xhi, xlo, True, True)
                    if w.turn:
                        pe.wait_ge(z_ok, k)
                    product(PZ, wh, 1, xhi, xlo, True, False)
                    if w.out:
                        pe.wait_ge(h_ok, k - 1)
                        if w.out == "leave" and not (isinstance(w.visit, int) and w.visit == 0):
                            pe.wait_ge(sum_ok, w.visit)
                        if w.out == "step" and s == 2 and isinstance(w.l, int) and w.l == 0 and not (
                                isinstance(w.sg, int) and w.sg == 0):
                            pe.wait_ge(sum_ok, w.visit)
                        turn(PT, lambda q: hT[:, w.old, q * 128:(q + 1) * 128]).then_inc(T_ps if w.out == "step" else F_ps, 1)
                    if w.enter:
                        pe.wait_ge(a_ok, CHUNKS)
                        pe.wait_ge(x2_ok, w.visit + SLOTS + 1)
                        pe.wait_ge(hi_ok, k + 2)
                        turn(PX, lambda q: nat[:, w.old, q, :]).then_inc(X_ps, 1)
                    if s == 0:
                        pe.wait_ge(wcur_ok, w.sg * LAYERS + w.l + 1)
                    pe.wait_ge(ghi_ok, k + 1)
                    pe.wait_ge(glo_ok, k + 1)
                    xhi, xlo = ghi[:, s, :], glo[:, s, :]
                    product(PR, wcur, 0, xhi, xlo, False, True).then_inc(r_ps, 1)
                    if w.turn:
                        pe.wait_ge(c_ok, k)
                    product(PI, wcur, 2, xhi, xlo, True, True).then_inc(i_ps, 1)
                    product(PZ, wcur, 1, xhi, xlo, False, True).then_inc(z_ps, 1)
                    if w.feed:
                        if w.out == "step":
                            pe.wait_ge(nat_ok, w.turned + 1)
                        aggregate(w.old, w.batch, s % 2)
                else:
                    for slot, bank in ((SLOTS - 2, PT), (SLOTS - 1, PX)):
                        pe.wait_ge(h_ok, STEPS * CHUNKS - SLOTS + slot + 1)
                        pe.wait_ge(sum_ok, (CHUNKS - 1) * SLOTS + slot - 1 if bank is PX else B // SB - 2)
                        turn(bank, lambda q: hT[:, slot, q * 128:(q + 1) * 128]).then_inc(F_ps, 1)


_INS = ["x", "adj", "nodemask", "L0_gnn_W1", "L0_gnn_b1", "L0_gnn_W2", "L0_gnn_b2", "L0_gnn_fusion_w",
        "L1_gnn_weight", "L1_gnn_w_ih", "L1_gnn_w_hh", "L1_gnn_b_ih", "L1_gnn_b_hh"]


def kernel(**inputs):
    import numpy as _np
    import concourse.bacc as _bacc
    from concourse import mybir as _mybir
    from concourse.bass_utils import run_bass_kernel_spmd as _run

    nc = _bacc.Bacc("TRN2", target_bir_lowering=False, num_devices=1)
    arrays, args = {}, []
    for name in _INS:
        a = _np.ascontiguousarray(inputs[name])
        arrays[f"in_{name}_dram"] = a
        args.append(nc.dram_tensor(f"in_{name}_dram", a.shape, _mybir.dt.from_np(a.dtype), kind="ExternalInput").ap())
    args.append(nc.dram_tensor("out_0_dram", (B, N, D), _mybir.dt.float32, kind="ExternalOutput").ap())
    build(nc, *args)
    r = _run(nc, [arrays], core_ids=[0])
    return r.results[0]["out_0_dram"]
```

```python
import concourse.bass as bass
from concourse import mybir
from contextlib import ExitStack

B, N, D = 64, 128, 128
GROUPS = [list(range(25)), [0, 1, 2, 3, 4, 5, 6, 7, 8], [0, 9, 10, 11, 12, 13, 14],
          [6, 7, 8, 12, 13, 14], [3, 4, 5, 9, 10, 11]]
NG = len(GROUPS)
FN = 25
HID = 256
HC = HID // 128
LAYERS = 5
GATES = 3 * D
EPS = 1e-5

CB = 16
CHUNKS = B // CB
SB = 4
SLOTS = CB // SB
COLS = SB * N
STEPS = LAYERS * SLOTS

TILES = [(0, 4, b) for b in range(0, CB, 4)] + [(1, 8, 0), (1, 8, 8)] + [(g, 16, 0) for g in (2, 3, 4)]
NT = len(TILES)
ROWS = [len(GROUPS[g]) * k for g, k, _ in TILES]
TA = [t for t in range(NT) if TILES[t][0] == 0]
TB = [t for t in range(NT) if TILES[t][0] != 0]
OFF = {}
for half in (TA, TB):
    at = 0
    for t in half:
        OFF[t] = at
        at += ROWS[t]
COLS_A, COLS_B = sum(ROWS[t] for t in TA), sum(ROWS[t] for t in TB)


def runs(nodes):
    out = []
    for i, v in enumerate(nodes):
        if out and v == out[-1][1] + out[-1][2]:
            out[-1][2] += 1
        else:
            out.append([i, v, 1])
    return [tuple(r) for r in out]


class Window:

    def __init__(self, sg, l, slot, turn, out, enter=False, stats1=None, apply1=None, stats2=None, apply2=None):
        self.sg, self.l, self.slot, self.turn, self.out, self.enter = sg, l, slot, turn, out, enter
        self.stats1, self.apply1, self.stats2, self.apply2 = stats1, apply1, stats2, apply2
        self.feed = out == "step" or enter
        self.k = sg * STEPS + l * SLOTS + slot
        self.prev = (slot - 1) % SLOTS
        self.old = (slot - 2) % SLOTS
        self.visit = sg * SLOTS + slot - 2
        self.turned = sg * (STEPS - SLOTS) + l * SLOTS + slot - 2
        self.batch = (self.visit + SLOTS) * SB if enter else sg * CB + self.old * SB


def opening(sg, first=False):
    return Window(sg, 0, 0, None if first else "leave", None if first else "leave", enter=not first)


def supergroup(eng, sg, first=False, more=True):
    left, coming = (sg - 1) * SLOTS, (sg + 1) * SLOTS
    halves, every = (range(SB // 2), range(SB // 2, SB)), range(SB)

    def norms(l, slot):
        out = {}
        if more and not (isinstance(l, int) and l == 0):
            out["stats1" if slot < 2 else "apply1"] = (coming + l - 1, halves[slot % 2])
        if not first:
            if slot >= 2 and not (isinstance(l, int) and l == LAYERS - 1):
                out["stats2"] = (left + l, l, halves[slot % 2])
            if slot < 2 and not (isinstance(l, int) and l == 0):
                out["apply2"] = (left + l - 1, l - 1, halves[slot % 2])
        return out

    for slot in range(1, SLOTS):
        yield Window(sg, 0, slot, "step", "step" if slot >= 2 else None if first else "leave",
                     enter=slot == 1 and not first, **norms(0, slot))
    with eng.Fori(1, LAYERS - 1) as l:
        for slot in range(SLOTS):
            yield Window(sg, l, slot, "step", "step", **norms(l, slot))
    for slot in range(SLOTS):
        share = norms(LAYERS - 1, slot)
        if not more and slot >= 2:
            share["stats2"] = (sg * SLOTS + slot - 2, slot - 2, every)
        if not more and slot == 3:
            share["apply2"] = (sg * SLOTS, 0, every)
        yield Window(sg, LAYERS - 1, slot, "leave" if slot else "step", "leave" if slot >= 2 else "step",
                     enter=more and slot >= 2, **share)


def windows(eng):
    yield opening(0, first=True)
    yield from supergroup(eng, 0, first=True)
    yield opening(1)
    with eng.Fori(1, CHUNKS - 1) as sg:
        yield from supergroup(eng, sg)
        yield opening(sg + 1)
    yield from supergroup(eng, CHUNKS - 1, more=False)
    yield None


def build(nc, x, adj, nodemask, W1, b1, W2, b2, fusion_w, weight, w_ih, w_hh, b_ih, b_hh, out):
    f32, f32r = mybir.dt.float32, mybir.dt.float32r
    ALU, ACT, AX = mybir.AluOpType, mybir.ActivationFunctionType, mybir.AxisListType
    ctx = ExitStack()
    with ctx:
        ctx.enter_context(nc.allow_non_contiguous_dma(reason="small rows of the adjacency"))

        def sb(name, shape, dt=f32):
            return ctx.enter_context(nc.sbuf_tensor(name, shape, dt))

        def sem(name):
            return ctx.enter_context(nc.semaphore(name))

        xn = sb("xn", [128, B, D])
        an = sb("an", [128, B, N])
        ident = sb("ident", [128, 128])
        w1 = sb("w1", [128, NG, HID])
        w2 = sb("w2", [128, NG, HC, D])
        rows = sb("rows", [NG * HC + NG + 6, 128])
        biasc = sb("biasc", [128, NG * HC + NG + 6])
        maskr = sb("maskr", [B, N])
        maskc = sb("maskc", [128, B])
        wh = sb("wh", [128, 2, GATES], f32r)
        wf = sb("wf", [128, LAYERS, 2, GATES], f32r)
        wcur = sb("wcur", [128, 2, GATES], f32r)
        gb = sb("gb", [128, 2])
        fw = sb("fw", [128, NG])
        fmx = sb("fmx", [128, 1])
        fsum = sb("fsum", [128, 1])
        fb2 = sb("fb2", [128, NG])
        ac = sb("ac", [128, CHUNKS, NT, FN])
        member = sb("member", [128, NT, FN])
        unit = sb("unit", [128, NT, FN])
        ksel = {k: sb(f"ksel{k}", [128, k]) for k in (4, 8, 16)}
        am = sb("am", [128, NT, FN])
        deg = sb("deg", [128, NT])
        zero = sb("zero", [128, NT])
        dinv = sb("dinv", [128, CHUNKS, NT])
        minus_half = sb("minus_half", [128, NT])
        tile_data = sb("tile_data", [128, 2 * NT * D])
        xt = tile_data[:, 0:NT * D].rearrange("p (t d) -> p t d", t=NT)
        s2 = tile_data[:, NT * D:].rearrange("p (t d) -> p t d", t=NT)
        bda = sb("bda", [128, COLS_A])
        bdb = sb("bdb", [128, COLS_B])
        na = sb("na", [128, COLS_A])
        nb = sb("nb", [128, COLS_B])
        ya = sb("ya", [128, COLS_A])
        yb = sb("yb", [128, COLS_B])
        ha = sb("ha", [128, HC, COLS_A])
        hb = sb("hb", [128, HC, COLS_B])
        fused = sb("fused", [128, CB * FN + 128])
        part = sb("part", [128, COLS_B])
        hT = sb("hT", [128, SLOTS, COLS])
        hhi = sb("hhi", [128, SLOTS, COLS], f32r)
        hlo = sb("hlo", [128, SLOTS, COLS], f32r)
        nat = sb("nat", [128, SLOTS, SB, D])
        ghi = sb("ghi", [128, SLOTS, COLS], f32r)
        glo = sb("glo", [128, SLOTS, COLS], f32r)
        rg = sb("rg", [128, 2, COLS])
        zg = sb("zg", [128, 2, COLS])
        cg = sb("cg", [128, 2, COLS])
        ng = sb("ng", [128, 2, COLS])
        dg = sb("dg", [128, 2, COLS])
        wir = rg[:, 0, 0:GATES].rearrange("p (c d) -> p c d", c=3)
        whr = rg[:, 1, 0:GATES].rearrange("p (c d) -> p c d", c=3)
        wl = zg[:].rearrange("p o (l d) -> p (o l) d", d=D)[:, 0:LAYERS, :]
        wlt = cg[:].rearrange("p o (l d) -> p (o l) d", d=D)[:, 0:LAYERS, :]
        wit = ng[:, 0, 0:GATES]
        yo = tile_data[:, 0:SLOTS * SB * D].rearrange("p (b d) -> p b d", d=D)
        st1, ag1, rs1, nm1 = sb("st1", [128, SB, 6]), sb("ag1", [128, SB, 2]), sb("rs1", [128, SB]), sb("nm1", [128, SB])
        st2, ag2 = sb("st2", [128, SLOTS, SB, 6]), sb("ag2", [128, SLOTS, SB, 2])
        rs2, nm2 = sb("rs2", [128, SLOTS, SB]), sb("nm2", [128, SLOTS, SB])

        def kept(visit):
            return visit % SLOTS if isinstance(visit, int) and visit >= B // SB - SLOTS else 0

        P = [ctx.enter_context(nc.psum_tensor(f"p{i}", [128, 512], f32)) for i in range(8)]
        PR, PH, PZ, PI, PT, PX = P[:6]
        PG = P[6:8]

        def b1c(g, c):
            return biasc[:, g * HC + c:g * HC + c + 1]
        BI = NG * HC + NG
        bin_, bhn = biasc[:, BI + 2:BI + 3], biasc[:, BI + 5:BI + 6]

        w_in, wl_in, w1_in, w2_in, xt_in, xt_pool_in, xa_in = map(sem, (
            "w_in", "wl_in", "w1_in", "w2_in", "xt_in", "xt_pool_in", "xa_in"))
        ac0_in, ac1_in, ac_in, ac0_pool_in, ac1_pool_in, ac_pool_in = map(sem, (
            "ac0_in", "ac1_in", "ac_in", "ac0_pool_in", "ac1_pool_in", "ac_pool_in"))
        wlt_ok, o2_ps = sem("wlt_ok"), sem("o2_ps")
        ident_ok, ac_zero, dve_c, pool_c, exp_ok = map(sem, ("ident_ok", "ac_zero", "dve_c", "pool_c", "exp_ok"))
        prep_t, prep_a, prep_f, prep_hi, prep_lo, fw_ok, b_ok = map(sem, (
            "prep_t", "prep_a", "prep_f", "prep_hi", "prep_lo", "fw_ok", "b_ok"))
        prep_c, deg_ok, pow_ok, am_ok, bd_ok = map(sem, ("prep_c", "deg_ok", "pow_ok", "am_ok", "bd_ok"))
        t_ps, y_ps, h_ps, s_ps, o_ps, f_ps = map(sem, ("t_ps", "y_ps", "h_ps", "s_ps", "o_ps", "f_ps"))
        na_ok, nb_ok, ya_ok, yb_ok, ha_ok, hb0_ok, hb1_ok, sa_ok, sb_ok, oa_ok, ob_ok, x_ok, a_ok = map(sem, (
            "na_ok", "nb_ok", "ya_ok", "yb_ok", "ha_ok", "hb0_ok", "hb1_ok", "sa_ok", "sb_ok", "oa_ok", "ob_ok", "x_ok", "a_ok"))
        r_ps, i_ps, z_ps, T_ps, X_ps, F_ps, G_ps = map(sem, ("r_ps", "i_ps", "z_ps", "T_ps", "X_ps", "F_ps", "G_ps"))
        r_ok, z_ok, n_ok, t1_ok, c_ok, d_ok, e_ok, h_ok = map(sem, ("r_ok", "z_ok", "n_ok", "t1_ok", "c_ok", "d_ok", "e_ok", "h_ok"))
        hi_ok, lo_ok, nat_ok, ghi_ok, glo_ok, wcur_ok = map(sem, (
            "hi_ok", "lo_ok", "nat_ok", "ghi_ok", "glo_ok", "wcur_ok"))
        bn1, ln1_st, ln1_rs, ln1_ok, x2_ok, sum_ok, bn2, ln2_st, ln2_rs, ln2_ok, out_ok = map(sem, (
            "bn1", "ln1_st", "ln1_rs", "ln1_ok", "x2_ok", "sum_ok", "bn2", "ln2_st", "ln2_rs", "ln2_ok", "out_ok"))
        yo_free, gathered, dev1, dev2 = map(sem, ("yo_free", "gathered", "dev1", "dev2"))
        waited = sem("waited")

        block = ctx.enter_context(nc.Block())

        def tile_rows(dram, c, t):
            g, k, b0 = TILES[t]
            for i, v, n in runs(GROUPS[g]):
                yield i * k, n * k, dram[bass.ds(c * CB + b0, k), v:v + n, :].rearrange("k n d -> n k d")

        def load_adj_rows(eng, c, done, tiles):
            for t in tiles:
                for r0, n, src in tile_rows(adj, c, t):
                    eng.dma_start(ac[r0:r0 + n, bass.ds(c, 1), t, :].rearrange("p o m -> p (o m)"),
                                  src[:, :, 0:FN]).then_inc(done, 16)

        def load_x_rows(eng, c, tiles, done):
            for t in tiles:
                for r0, n, src in tile_rows(x, c, t):
                    eng.dma_start(xt[r0:r0 + n, t, :], src).then_inc(done, 16)

        def load_chunk(eng, c):
            for dst, src in ((xn, x), (an, adj)):
                for b in (0, CB // 2):
                    eng.dma_start(dst[:, bass.ds(c * CB + b, CB // 2), :],
                                  src[bass.ds(c * CB + b, CB // 2), :, :].rearrange("b n d -> n b d")).then_inc(xa_in, 16)

        def group_cols(g):
            mine = [t for t in TB if TILES[t][0] == g]
            return OFF[mine[0]], OFF[mine[-1]] + ROWS[mine[-1]]

        X_BANKS = (PX, P[0])
        WF_BANKS = (5, 4, 6, 7, 0)
        F_BANKS, F_BANKS_LAST = (2, 5, 3, 4), (1, 2, 3, 4)

        def n_runs(tiles):
            return sum(len(runs(GROUPS[TILES[t][0]])) for t in tiles)
        ADDS = n_runs(TB)
        XT_SP, XT_POOL = range(0, NT - 2), range(NT - 2, NT)

        def wait_alone(eng, signal, value):
            eng.wait_ge(signal, value)
            eng.sem_inc(waited, 1)

        @block.sync
        def _(sp):
            sp.wait_ge(ac_zero, 1)
            load_adj_rows(sp, 0, ac0_in, TB)
            for i, (name, src) in enumerate((("b1", b1.rearrange("g (c h) -> (g c) h", c=HC)), ("b2", b2),
                                             ("b_ih", b_ih.rearrange("(c h) -> c h", h=128)),
                                             ("b_hh", b_hh.rearrange("(c h) -> c h", h=128)))):
                r0 = (0, NG * HC, NG * HC + NG, NG * HC + NG + 3)[i]
                sp.dma_start(rows[r0:r0 + src.shape[0], :], src).then_inc(w_in, 16)
            sp.dma_start(maskr[:], nodemask).then_inc(w_in, 16)
            sp.dma_start(fw[:], fusion_w.partition_broadcast(128)).then_inc(w_in, 16)
            sp.dma_start(w1[:], W1.rearrange("g d h -> d g h")).then_inc(w1_in, 16)
            load_x_rows(sp, 0, XT_SP, xt_in)
            sp.dma_start(w2[:], W2.rearrange("g (c h) d -> h g c d", c=HC)).then_inc(w2_in, 16)
            sp.wait_ge(ac_zero, 2)
            load_adj_rows(sp, 1, ac1_in, TB)
            load_chunk(sp, 0)

            def load_x(c):
                sp.wait_ge(y_ps, 2 * c - 1)
                load_x_rows(sp, c, TA, xt_in)
                sp.wait_ge(y_ps, 2 * c)
                load_x_rows(sp, c, [t for t in XT_SP if t not in TA], xt_in)

            with sp.Fori(1, CHUNKS - 1) as c:
                load_x(c)
                load_adj_rows(sp, c + 1, ac_in, TB)
                sp.wait_ge(xa_in, 64 * c)
                load_chunk(sp, c)
                wait_alone(sp, ac_in, 16 * n_runs(TB) * c)
            load_x(CHUNKS - 1)
            sp.wait_ge(xa_in, 64 * (CHUNKS - 1))
            load_chunk(sp, CHUNKS - 1)
            sp.sem_inc(yo_free, SLOTS)
            with sp.Fori(0, CHUNKS) as sg:
                for slot in range(SLOTS):
                    v = sg * SLOTS + slot
                    sp.wait_ge(ln2_ok, v + 1)
                    sp.dma_start(out[bass.ds(v * SB, SB), :, :].rearrange("b n d -> n b d"),
                                 yo[:, slot * SB:(slot + 1) * SB, :]).then_inc(out_ok, 16)
                    sp.wait_ge(out_ok, 16 * (v + 1))
                    sp.sem_inc(yo_free, 1)
            sp.wait_ge(out_ok, 16 * (B // SB))

        def counter(eng, signal):
            n = [0]

            def link(ins):
                n[0] += 1
                ins.then_inc(signal, 1)
                eng.wait_ge(signal, n[0])
            return link

        @block.gpsimd
        def _(pool):
            link = counter(pool, pool_c)
            nc.gpsimd.memset(ac[:, 0], 0.0).then_inc(ac_zero, 1)
            link(nc.gpsimd.memset(ident[:], 0.0))
            nc.gpsimd.affine_select(out=ident[:], in_=ident[:], compare_op=ALU.not_equal, fill=1.0, base=0,
                                    pattern=[[-1, 128]], channel_multiplier=1).then_inc(ident_ok, 1)
            nc.gpsimd.memset(fused[:], 0.0)
            nc.gpsimd.memset(ac[:, 1:], 0.0).then_inc(ac_zero, 1)
            link(nc.gpsimd.memset(minus_half[:], -0.5))

            def load_adj(c):
                if c > 2:
                    pool.wait_ge(ac_pool_in, 16 * n_runs(TA) * (c - 2))
                load_adj_rows(pool, c, (ac0_pool_in, ac1_pool_in, ac_pool_in, ac_pool_in)[c], TA)

            load_adj(0)
            load_x_rows(pool, 0, XT_POOL, xt_pool_in)

            def power(c):
                wait_alone(pool, deg_ok, c + 1)
                nc.gpsimd.tensor_tensor(dinv[:, bass.ds(c, 1), :].rearrange("p o t -> p (o t)"), deg[:], minus_half[:],
                                        ALU.pow).then_inc(pow_ok, 1)

            def spread(c):
                wait_alone(pool, am_ok, c + 1)
                for t0, nt, pieces in ((0, 4, [(0, 0, 1, 25)]), (4, 2, [(0, 0, 1, 9)]), (6, 1, [(0, 0, 1, 1), (1, 9, 1, 6)]),
                                       (7, 1, [(0, 6, 2, 3)]), (8, 1, [(0, 3, 2, 3)])):
                    k, r, o = TILES[t0][1], ROWS[t0], OFF[t0]
                    dst = bda if t0 == 0 else bdb
                    a_t = am[0:r, t0:t0 + nt, :]
                    for i, v, s, n in pieces:
                        src = a_t[:, :, v:v + n] if s == 1 else a_t[:, 0, v:v + 12].rearrange("p (s m) -> p s m", s=2)[:, :, 0:n]
                        a = nt * s
                        d = dst[0:r, o + i * k:o + i * k + a * n * k].rearrange("p (a m k) -> p a m k", a=a, k=k)
                        last = nc.gpsimd.tensor_tensor(
                            d, src.unsqueeze(3).to_broadcast([r, a, n, k]),
                            ksel[k][0:r, :].unsqueeze(1).unsqueeze(1).to_broadcast([r, a, n, k]), ALU.mult)
                last.then_inc(bd_ok, 1)

            def deviation(ag, rs, nm, done, visit):
                nc.gpsimd.tensor_scalar(rs, ag[:, :, 1], EPS, 1.0, ALU.add, ALU.mult).then_inc(done, 1)
                nc.gpsimd.tensor_scalar(nm, ag[:, :, 0], -1.0, 0.0, ALU.mult, ALU.add).then_inc(done, 1)
                pool.wait_ge(done, 3 * visit + 1)
                nc.gpsimd.tensor_tensor(rs, rs, minus_half[:, 0:SB], ALU.pow).then_inc(done, 1)
                pool.wait_ge(done, 3 * visit + 3)
                return nc.gpsimd.tensor_tensor(nm, nm, rs, ALU.mult)

            def deviation1(visit):
                wait_alone(pool, ln1_st, visit + 1)
                deviation(ag1, rs1[:], nm1[:], dev1, visit).then_inc(ln1_rs, 1)

            def deviation2(visit):
                wait_alone(pool, ln2_st, visit + 1)
                o = kept(visit)
                deviation(ag2[:, o], rs2[:, o], nm2[:, o], dev2, visit).then_inc(ln2_rs, 1)

            def prepare(c):
                pool.wait_ge(y_ps, 2 * c)
                load_x_rows(pool, c, XT_POOL[1:], xt_pool_in)
                power(c)
                pool.wait_ge(t_ps, 2 * c)
                spread(c)
                load_x_rows(pool, c, XT_POOL[:1], xt_pool_in)

            power(0)
            spread(0)
            load_adj(1)
            load_adj(2)
            prepare(1)
            load_adj(3)
            with pool.Fori(0, CHUNKS - 2) as c:
                prepare(c + 2)
                deviation1(c)
                wait_alone(pool, ln1_ok, c + 1)
            deviation1(2)
            pool.wait_ge(ln1_ok, 3)
            deviation1(3)
            for w in windows(pool):
                if w:
                    pool.wait_ge(n_ok, w.k + 1)
                    nc.gpsimd.tensor_tensor(dg[:, w.slot % 2, :], hT[:, w.slot, :], ng[:, w.slot % 2, :],
                                            ALU.subtract).then_inc(d_ok, 1)
                    if w.stats1 and SB - 1 in w.stats1[1]:
                        deviation1(w.stats1[0])
                    if w.stats2 and SB - 1 in w.stats2[2]:
                        deviation2(w.stats2[0])
                else:
                    for slot in range(2, SLOTS):
                        deviation2((CHUNKS - 1) * SLOTS + slot)

        @block.scalar
        def _(act):
            act.dma_start(wir, w_ih.rearrange("(c e) d -> e c d", c=3)).then_inc(wl_in, 16)
            act.dma_start(whr, w_hh.rearrange("(c e) d -> e c d", c=3)).then_inc(wl_in, 16)
            act.dma_start(wl, weight.rearrange("l c e -> c l e")).then_inc(wl_in, 16)
            act.wait_ge(prep_t, 1)
            nc.scalar.copy(wit, P[0][:, 0:GATES])
            act.wait_ge(prep_t, 2)
            nc.scalar.copy(wh[:, 0, :], P[1][:, 0:GATES]).then_inc(prep_hi, 1)
            act.wait_ge(prep_t, 3)
            nc.scalar.copy(wlt[:, 0:4, :], P[2][:].rearrange("p (l d) -> p l d", l=4))
            act.wait_ge(prep_t, 4)
            nc.scalar.copy(wlt[:, 4, :], P[3][:, 0:128]).then_inc(wlt_ok, 1)
            for l in range(LAYERS):
                act.wait_ge(prep_f, l + 1)
                nc.scalar.copy(wf[:, l, 0, :], P[WF_BANKS[l]][:, 0:GATES]).then_inc(prep_hi, 1)
            act.wait_ge(fw_ok, 1)
            nc.scalar.activation(fw[:], fw[:], ACT.Exp, bias=fmx[:], accum_out=fsum[:]).then_inc(exp_ok, 1)
            act.wait_ge(prep_t, 5)
            nc.scalar.copy(maskc[:], P[3][:, 256:256 + B])
            nc.scalar.copy(biasc[:], P[3][:, 128:128 + NG * HC + NG + 6]).then_inc(prep_a, 1)
            act.wait_ge(b_ok, 1)

            def adjacency(c):
                act.wait_ge(t_ps, 2 * c + 1)
                for t in TA:
                    if t == TA[2] and not (isinstance(c, int) and c == 0):
                        wait_alone(act, o_ps, 2 * c - 1)
                    r, o = ROWS[t], OFF[t]
                    dv = dinv[0:r, bass.ds(c, 1), t:t + 1].rearrange("p o t -> p (o t)")
                    last = nc.scalar.activation(na[0:r, o:o + r], P[2][0:r, o:o + r], ACT.Identity, scale=dv)
                last.then_inc(na_ok, 1)

            def neighbours(c):
                act.wait_ge(y_ps, 2 * c + 1)
                nc.scalar.copy(ya[:], P[2][:, 0:COLS_A]).then_inc(ya_ok, 1)

            def hidden(c):
                for h in range(HC):
                    act.wait_ge(h_ps, 4 * c + 1 + h)
                    nc.scalar.activation(ha[:, h, :], P[6 + h][:, 0:COLS_A], ACT.Relu, bias=b1c(0, h)).then_inc(ha_ok, 1)
                act.wait_ge(h_ps, 4 * c + 4)
                for g in range(1, NG):
                    a, b = group_cols(g)
                    last = nc.scalar.activation(hb[:, 1, a:b], P[1][:, a:b], ACT.Relu, bias=b1c(g, 1))
                last.then_inc(hb1_ok, 1)
                act.wait_ge(s_ps, 3 * c + 1)
                nc.scalar.copy(s2[0:ROWS[0], 0:4, :], P[6][0:ROWS[0], :].rearrange("p (t d) -> p t d", t=4)).then_inc(sa_ok, 1)

            def output_a(c):
                act.wait_ge(o_ps, 2 * c + 1)
                nc.scalar.activation(fused[:, 0:CB * FN].rearrange("p (t k n) -> p t n k", t=4, n=FN),
                                     P[3][:, 0:COLS_A].rearrange("p (t n k) -> p t n k", t=4, n=FN),
                                     ACT.Relu, bias=fb2[:, 0:1], scale=fw[:, 0:1]).then_inc(oa_ok, 1)

            def output_b(c):
                act.wait_ge(o_ps, 2 * c + 2)
                for g in range(1, NG):
                    a, b = group_cols(g)
                    last = nc.scalar.activation(part[:, a:b], P[4][:, a:b], ACT.Relu, bias=fb2[:, g:g + 1], scale=fw[:, g:g + 1])
                last.then_inc(ob_ok, 1)

            def norm1(visit, part=range(SB)):
                if 0 in part:
                    act.wait_ge(ln1_rs, visit + 1)
                for q in part:
                    xq = xn[:, bass.ds(visit * SB + q, 1), :].rearrange("p o d -> p (o d)")
                    last = nc.scalar.activation(xq, xq, ACT.Identity, bias=nm1[:, q:q + 1], scale=rs1[:, q:q + 1])
                if SB - 1 in part:
                    last.then_inc(ln1_ok, 1)

            def norm2(visit, slot, part=range(SB)):
                o = kept(visit)
                if 0 in part:
                    act.wait_ge(ln2_rs, visit + 1)
                for q in part:
                    yq = yo[:, bass.ds(slot * SB + q, 1), :].rearrange("p o d -> p (o d)")
                    last = nc.scalar.activation(yq, yq, ACT.Identity, bias=nm2[:, o, q:q + 1], scale=rs2[:, o, q:q + 1])
                if SB - 1 in part:
                    last.then_inc(ln2_ok, 1)

            def turn_over(c):
                wait_alone(act, o2_ps, 2 * c + 1)
                adjacency(c + 1)
                output_a(c)

            adjacency(0)
            neighbours(0)
            hidden(0)
            turn_over(0)
            with act.Fori(0, CHUNKS - 2) as c:
                neighbours(c + 1)
                output_b(c)
                hidden(c + 1)
                turn_over(c + 1)
                norm1(c)
            neighbours(CHUNKS - 1)
            output_b(CHUNKS - 2)
            norm1(2)
            hidden(CHUNKS - 1)
            norm1(3)
            output_a(CHUNKS - 1)
            output_b(CHUNKS - 1)

            def aggregated(m, s, par):
                act.wait_ge(G_ps, m + 1)
                nc.scalar.copy(ghi[:, s, :], PG[par][:]).then_inc(ghi_ok, 1)

            for s in range(SLOTS):
                act.wait_ge(X_ps, s + 1)
                nc.scalar.copy(hT[:, s, :], X_BANKS[s % 2][:])
                nc.scalar.copy(hhi[:, s, :], X_BANKS[s % 2][:]).then_inc(hi_ok, 1)
                aggregated(s, s, s % 2)
            for w in windows(act):
                if w:
                    k, s, p = w.k, w.slot, w.slot % 2
                    if w.enter:
                        act.wait_ge(G_ps, k - 1)
                        wait_alone(act, ln1_ok, w.visit + SLOTS + 1)
                        nc.scalar.activation(nat[:, w.old], xn[:, bass.ds(w.batch, SB), :], ACT.Identity).then_inc(x2_ok, 1)
                    if w.out == "step":
                        act.wait_ge(T_ps, w.turned + 1)
                        nc.scalar.copy(nat[:, w.old], PT[:].rearrange("p (b d) -> p b d", b=SB)).then_inc(nat_ok, 1)
                    act.wait_ge(r_ps, k + 1)
                    nc.scalar.activation(rg[:, p, :], PR[:], ACT.Sigmoid, bias=gb[:, 0:1]).then_inc(r_ok, 1)
                    if w.apply1:
                        norm1(*w.apply1)
                    if w.apply2:
                        norm2(*w.apply2)
                    if w.enter:
                        act.wait_ge(X_ps, w.visit + SLOTS + 1)
                        nc.scalar.copy(hT[:, w.old, :], PX[:])
                        nc.scalar.copy(hhi[:, w.old, :], PX[:]).then_inc(hi_ok, 1)
                    act.wait_ge(z_ps, k + 1)
                    nc.scalar.activation(zg[:, p, :], PZ[:], ACT.Sigmoid, bias=gb[:, 1:2]).then_inc(z_ok, 1)
                    act.wait_ge(c_ok, k + 1)
                    nc.scalar.activation(ng[:, p, :], cg[:, p, :], ACT.Tanh, bias=bin_).then_inc(n_ok, 1)
                    if w.feed:
                        aggregated(k + 2, w.old, s % 2)
                    if w.turn == "step":
                        act.wait_ge(h_ok, k)
                        nc.scalar.copy(hhi[:, w.prev, :], hT[:, w.prev, :]).then_inc(hi_ok, 1)
                else:
                    for slot in range(1, SLOTS):
                        norm2((CHUNKS - 1) * SLOTS + slot, slot)

        @block.vector
        def _(dve):
            link = counter(dve, dve_c)
            TT, TS, STT = nc.vector.tensor_tensor, nc.vector.tensor_scalar, nc.vector.scalar_tensor_tensor
            link(nc.vector.memset(member[:], 0.0))
            link(nc.vector.memset(unit[:], 0.0))
            dve.wait_ge(ident_ok, 1)
            for t, (g, k, _) in enumerate(TILES):
                for i, v, n in runs(GROUPS[g]):
                    nc.vector.memset(member[:, t, v:v + n], 1.0)
                    nc.vector.reduce_sum(unit[:, t, v:v + n],
                                         ident[:, i * k:(i + n) * k].rearrange("p (n k) -> p n k", k=k), AX.X)
            for k in ksel:
                last = nc.vector.reduce_sum(ksel[k][:], ident[:].rearrange("p (n k) -> p k n", k=k), AX.X)
            link(last)

            def degrees(c):
                if not isinstance(c, int) or c:
                    dve.wait_ge(bd_ok, c)
                if isinstance(c, int):
                    dve.wait_ge((ac0_pool_in, ac1_pool_in)[c], 16 * n_runs(TA))
                    wait_alone(dve, (ac0_in, ac1_in)[c], 16 * n_runs(TB))
                else:
                    wait_alone(dve, ac_pool_in, 16 * n_runs(TA) * (c - 1))
                    wait_alone(dve, ac_in, 16 * n_runs(TB) * (c - 1))
                flat = am[:].rearrange("p t m -> p (t m)")
                TT(flat, ac[:, bass.ds(c, 1)].rearrange("p o t m -> p (o t m)"), member[:].rearrange("p t m -> p (t m)"),
                   ALU.mult).then_inc(prep_c, 1)
                dve.wait_ge(prep_c, 6 * c + 1)
                TT(flat, flat, unit[:].rearrange("p t m -> p (t m)"), ALU.add).then_inc(prep_c, 1)
                wait_alone(dve, prep_c, 6 * c + 2)
                nc.vector.reduce_sum(deg[:], am[:], AX.X).then_inc(prep_c, 1)
                wait_alone(dve, prep_c, 6 * c + 3)
                TS(zero[:], deg[:], 0.0, None, ALU.is_equal).then_inc(prep_c, 1)
                dve.wait_ge(prep_c, 6 * c + 4)
                TT(deg[:], deg[:], zero[:], ALU.add).then_inc(deg_ok, 1)
                TS(zero[:], zero[:], -1.0, 1.0, ALU.mult, ALU.add).then_inc(prep_c, 1)

            def scaled(c):
                dve.wait_ge(pow_ok, c + 1)
                wait_alone(dve, prep_c, 6 * c + 5)
                dv = dinv[:, bass.ds(c, 1), :].rearrange("p o t -> p (o t)")
                TT(dv, dv, zero[:], ALU.mult).then_inc(prep_c, 1)
                dve.wait_ge(prep_c, 6 * c + 6)
                TT(am[:], am[:], dv.unsqueeze(2).to_broadcast([128, NT, FN]), ALU.mult).then_inc(am_ok, 1)

            degrees(0)
            dve.wait_ge(prep_hi, 1)
            TT(wh[:, 1, :], P[1][:, 0:GATES], wh[:, 0, :], ALU.subtract)
            scaled(0)
            for l in range(LAYERS):
                dve.wait_ge(prep_hi, l + 2)
                TT(wf[:, l, 1, :], P[WF_BANKS[l]][:, 0:GATES], wf[:, l, 0, :], ALU.subtract).then_inc(prep_lo, 1)
            dve.wait_ge(w_in, 16 * 6)
            nc.vector.tensor_reduce(fmx[:], fw[:], AX.X, ALU.max, negate=True).then_inc(fw_ok, 1)
            dve.wait_ge(exp_ok, 1)
            link(nc.vector.reciprocal(fsum[:], fsum[:]))
            link(TS(fw[:], fw[:], fsum[:], None, ALU.mult))
            dve.wait_ge(prep_a, 1)
            TT(gb[:], biasc[:, BI:BI + 2], biasc[:, BI + 3:BI + 5], ALU.add)
            TT(fb2[:], biasc[:, NG * HC:BI], fw[:], ALU.mult).then_inc(b_ok, 1)

            def adjacency(c):
                dve.wait_ge(t_ps, 2 * c + 2)
                for t in TB:
                    if t == TB[2] and not (isinstance(c, int) and c == 0):
                        wait_alone(dve, o_ps, 2 * c)
                    r, o = ROWS[t], OFF[t]
                    dv = dinv[0:r, bass.ds(c, 1), t:t + 1].rearrange("p o t -> p (o t)")
                    last = TS(nb[0:r, o:o + r], P[5][0:r, o:o + r], dv, None, ALU.mult)
                last.then_inc(nb_ok, 1)

            def neighbours(c):
                dve.wait_ge(y_ps, 2 * c + 2)
                nc.vector.tensor_copy(yb[:], P[5][:, 0:COLS_B]).then_inc(yb_ok, 1)

            def hidden(c):
                dve.wait_ge(h_ps, 4 * c + 3)
                for g in range(1, NG):
                    a, b = group_cols(g)
                    last = TS(hb[:, 0, a:b], P[0][:, a:b], b1c(g, 0), 0.0, ALU.add, ALU.max)
                last.then_inc(hb0_ok, 1)

            def second(c):
                dve.wait_ge(s_ps, 3 * c + 2)
                nc.vector.tensor_copy(s2[0:ROWS[4], 4:6, :], P[7][0:ROWS[4], 0:256].rearrange("p (t d) -> p t d", t=2))
                dve.wait_ge(s_ps, 3 * c + 3)
                nc.vector.tensor_copy(s2[0:ROWS[6], 6, :], P[0][0:ROWS[6], 0:128])
                nc.vector.tensor_copy(s2[0:ROWS[7], 7:9, :], P[0][0:ROWS[7], 128:384].rearrange("p (t d) -> p t d", t=2)).then_inc(sb_ok, 1)

            def gather(c):
                dve.wait_ge(oa_ok, c + 1)
                wait_alone(dve, ob_ok, c + 1)
                f = fused[:, 0:CB * FN].rearrange("p (b n) -> p b n", n=FN)
                n_add = 0
                for t in TB:
                    g, k, b0 = TILES[t]
                    for i, v, n in runs(GROUPS[g]):
                        d = f[:, b0:b0 + k, v:v + n]
                        s = part[:, OFF[t] + i * k:OFF[t] + (i + n) * k].rearrange("p (n k) -> p k n", k=k)
                        if n_add:
                            dve.wait_ge(gathered, ADDS * c + n_add)
                        n_add += 1
                        TT(d, d, s, ALU.add).then_inc(gathered, 1)

            def add(c, banks):
                dve.wait_ge(xa_in, 64 * c + 64)
                for q in range(4):
                    wait_alone(dve, f_ps, 4 * c + q + 1)
                    xq = xn[0:FN, bass.ds(c * CB + q * 4, 4), :]
                    TT(xq, xq, P[banks[q]][0:FN, :].rearrange("p (b d) -> p b d", b=4), ALU.add).then_inc(x_ok, 1)

            def ones(c):
                dve.wait_ge(xa_in, 64 * c + 64)
                ab = an[:, bass.ds(c * CB, CB), :]
                TS(ab, ab, 0.0, None, ALU.not_equal).then_inc(a_ok, 1)

            def norm1(visit, part=range(SB)):
                for q in part:
                    last = nc.vector.bn_stats(st1[:, q, :], xn[:, bass.ds(visit * SB + q, 1), :].rearrange("p o d -> p (o d)"))
                if SB - 1 not in part:
                    return
                last.then_inc(bn1, 1)
                wait_alone(dve, bn1, visit + 1)
                for q in range(SB):
                    last = nc.vector.bn_aggr(ag1[:, q, :], st1[:, q, :])
                last.then_inc(ln1_st, 1)

            def settle(s, b, ready):
                wait_alone(dve, ln1_ok, ready)
                nc.vector.tensor_copy(nat[:, s], xn[:, bass.ds(b, SB), :]).then_inc(x2_ok, 1)

            adjacency(0)
            neighbours(0)
            degrees(1)
            hidden(0)
            scaled(1)
            second(0)

            def chunk(c, more):
                wait_alone(dve, o2_ps, 2 * c + 2)
                adjacency(c + 1)
                if more:
                    degrees(c + 2)
                else:
                    norm1(c)
                neighbours(c + 1)
                gather(c)
                hidden(c + 1)
                if more:
                    scaled(c + 2)
                else:
                    dve.wait_ge(ln1_rs, c + 1)
                    norm1(c + 1)
                add(c, F_BANKS)
                if more:
                    wait_alone(dve, x_ok, 4)
                    norm1(c)
                second(c + 1)
                if more:
                    ones(c)
                    wait_alone(dve, ln1_rs, c + 1)

            with dve.Fori(0, CHUNKS - 2) as c:
                chunk(c, True)
            chunk(CHUNKS - 2, False)
            for s in range(SLOTS):
                settle(s, s * SB, s + 1)
            gather(CHUNKS - 1)

            def lo_state(m, s):
                dve.wait_ge(hi_ok, m + 1)
                TT(hlo[:, s, :], hT[:, s, :], hhi[:, s, :], ALU.subtract).then_inc(lo_ok, 1)

            def lo_neighbours(m, s, par):
                dve.wait_ge(ghi_ok, m + 1)
                TT(glo[:, s, :], PG[par][:], ghi[:, s, :], ALU.subtract).then_inc(glo_ok, 1)

            def layer_weights(l):
                nc.vector.tensor_copy(wcur[:], wf[:, bass.ds(l, 1)].rearrange("p o h e -> p (o h) e")).then_inc(wcur_ok, 1)

            lo_state(0, 0)
            lo_neighbours(0, 0, 0)
            lo_neighbours(1, 1, 1)
            add(CHUNKS - 1, F_BANKS_LAST)
            layer_weights(0)
            lo_state(1, 1)
            for s in range(2, SLOTS):
                lo_state(s, s)
                lo_neighbours(s, s, s % 2)

            def end_step(k, s):
                dve.wait_ge(d_ok, k)
                TT(dg[:, s % 2, :], zg[:, s % 2, :], dg[:, s % 2, :], ALU.mult).then_inc(e_ok, 1)
                dve.wait_ge(e_ok, k)
                TT(hT[:, s, :], ng[:, s % 2, :], dg[:, s % 2, :], ALU.add).then_inc(h_ok, 1)

            def leave(visit, slot, bank):
                dve.wait_ge(F_ps, visit + 1)
                dve.wait_ge(yo_free, visit + 1)
                for q in range(SB):
                    b = visit * SB + q
                    last = STT(yo[:, slot * SB + q, :], bank[:, q * D:(q + 1) * D], maskc[:, bass.ds(b, 1)],
                               xn[:, bass.ds(b, 1), :].rearrange("p o d -> p (o d)"), ALU.mult, ALU.add)
                last.then_inc(sum_ok, 1)

            def norm2(visit, slot, part=range(SB)):
                o = kept(visit)
                if o == 0 and 0 in part:
                    wait_alone(dve, yo_free, visit + SLOTS)
                dve.wait_ge(sum_ok, visit + 1)
                for q in part:
                    last = nc.vector.bn_stats(st2[:, o, q, :], yo[:, bass.ds(slot * SB + q, 1), :].rearrange("p o d -> p (o d)"))
                if SB - 1 not in part:
                    return
                last.then_inc(bn2, 1)
                wait_alone(dve, bn2, visit + 1)
                for q in range(SB):
                    last = nc.vector.bn_aggr(ag2[:, o, q, :], st2[:, o, q, :])
                last.then_inc(ln2_st, 1)

            for w in windows(dve):
                if w:
                    k, s, p = w.k, w.slot, w.slot % 2
                    if w.out == "leave":
                        leave(w.visit, w.old, PT)
                    dve.wait_ge(r_ok, k + 1)
                    STT(cg[:, p, :], PH[:], bhn, rg[:, p, :], ALU.add, ALU.mult).then_inc(t1_ok, 1)
                    dve.wait_ge(i_ps, k + 1)
                    dve.wait_ge(t1_ok, k + 1)
                    TT(cg[:, p, :], cg[:, p, :], PI[:], ALU.add).then_inc(c_ok, 1)
                    if w.turn:
                        end_step(k, w.prev)
                    last_layer = isinstance(w.l, int) and w.l == LAYERS - 1
                    if s == SLOTS - 1 and not (last_layer and not w.enter):
                        wait_alone(dve, z_ps, k + 1)
                        layer_weights(0 if last_layer else w.l + 1)
                    if w.stats1:
                        dve.wait_ge(ln1_ok, w.stats1[0])
                        norm1(*w.stats1)
                    if w.stats2:
                        norm2(*w.stats2)
                    if w.enter:
                        lo_state(k + 2, w.old)
                    if w.feed:
                        lo_neighbours(k + 2, w.old, s % 2)
                    if w.turn == "step":
                        lo_state(k + 3, w.prev)
                    if isinstance(k, int) and 2 <= k < CHUNKS:
                        ones(k)
                else:
                    last = B // SB - 1
                    leave(last - 1, SLOTS - 2, PT)
                    end_step(B // SB * LAYERS, SLOTS - 1)
                    norm2(last - 1, SLOTS - 2)
                    leave(last, SLOTS - 1, PX)
                    norm2(last, SLOTS - 1)

        @block.tensor
        def _(pe):
            MM, TR = nc.tensor.matmul, nc.tensor.transpose
            pe.wait_ge(ident_ok, 1)
            pe.wait_ge(wl_in, 48)
            for i in range(3):
                last = TR(P[0][:, i * 128:(i + 1) * 128], wir[:, i, :], ident[:])
            last.then_inc(prep_t, 1)
            for i in range(3):
                last = TR(P[1][:, i * 128:(i + 1) * 128], whr[:, i, :], ident[:])
            last.then_inc(prep_t, 1)
            for l in range(4):
                last = TR(P[2][:, l * 128:(l + 1) * 128], wl[:, l, :], ident[:])
            last.then_inc(prep_t, 1)
            TR(P[3][:, 0:128], wl[:, 4, :], ident[:]).then_inc(prep_t, 1)
            pe.wait_ge(wlt_ok, 1)
            for l in range(LAYERS):
                MM(P[WF_BANKS[l]][:, 0:GATES], wlt[:, l, :], wit, start=True, stop=True).then_inc(prep_f, 1)
            pe.wait_ge(w_in, 16 * 6)
            nr = NG * HC + NG + 6
            TR(P[3][:, 128:128 + nr], rows[:], ident[0:nr, 0:nr])
            TR(P[3][:, 256:256 + B], maskr[:], ident[0:B, 0:B]).then_inc(prep_t, 1)
            pe.wait_ge(prep_lo, 1)

            def adjacency(c):
                pe.wait_ge(bd_ok, c + 1)
                for half, bd, bank in ((TA, bda, 2), (TB, bdb, 5)):
                    for t in half:
                        r, o = ROWS[t], OFF[t]
                        last = TR(P[bank][0:r, o:o + r], bd[0:r, o:o + r], ident[0:r, 0:r])
                    last.then_inc(t_ps, 1)

            def first(c):
                pe.wait_ge(xt_in, 16 * n_runs(XT_SP) * (c + 1))
                pe.wait_ge(xt_pool_in, 16 * n_runs(XT_POOL) * (c + 1))
                for half, nn, bank, ready in ((TA, na, 2, na_ok), (TB, nb, 5, nb_ok)):
                    pe.wait_ge(ready, c + 1)
                    for t in half:
                        r, o = ROWS[t], OFF[t]
                        last = MM(P[bank][:, o:o + r], xt[0:r, t, :], nn[0:r, o:o + r], start=True, stop=True)
                    last.then_inc(y_ps, 1)
                if isinstance(c, int):
                    pe.wait_ge(w1_in, 16)
                    pe.wait_ge(prep_lo, LAYERS)
                pe.wait_ge(ya_ok, c + 1)
                for h in range(HC):
                    MM(P[6 + h][:, 0:COLS_A], w1[:, 0, h * 128:(h + 1) * 128], ya[:], start=True, stop=True).then_inc(h_ps, 1)
                pe.wait_ge(yb_ok, c + 1)
                for h in range(HC):
                    for g in range(1, NG):
                        a, b = group_cols(g)
                        last = MM(P[h][:, a:b], w1[:, g, h * 128:(h + 1) * 128], yb[:, a:b], start=True, stop=True)
                    last.then_inc(h_ps, 1)

            def times_w2(tiles, hid, bank):
                for i, t in enumerate(tiles):
                    g, r, o = TILES[t][0], ROWS[t], OFF[t]
                    for h in range(HC):
                        last = MM(P[bank][0:r, i * D:(i + 1) * D], hid[:, h, o:o + r], w2[:, g, h, :],
                                  start=(h == 0), stop=(h == HC - 1))
                last.then_inc(s_ps, 1)

            def second(c):
                pe.wait_ge(ha_ok, 2 * c + 2)
                times_w2(TA, ha, 6)
                pe.wait_ge(hb0_ok, c + 1)
                pe.wait_ge(hb1_ok, c + 1)
                times_w2(TB[0:2], hb, 7)
                times_w2(TB[2:5], hb, 0)

            def output(c):
                for half, nn, bank, ready in ((TA, na, 3, sa_ok), (TB, nb, 4, sb_ok)):
                    pe.wait_ge(ready, c + 1)
                    for t in half:
                        r, o = ROWS[t], OFF[t]
                        last = MM(P[bank][:, o:o + r], s2[0:r, t, :], nn[0:r, o:o + r], start=True, stop=True)
                        if t == half[1]:
                            last.then_inc(o2_ps, 1)
                    last.then_inc(o_ps, 1)

            def back(c, banks):
                pe.wait_ge(gathered, ADDS * (c + 1))
                for q in range(4):
                    for i in range(4):
                        b = 4 * q + i
                        last = TR(P[banks[q]][:, i * D:(i + 1) * D], fused[:, b * FN:b * FN + 128], ident[:])
                    last.then_inc(f_ps, 1)

            adjacency(0)
            first(0)
            pe.wait_ge(w2_in, 16)
            second(0)
            with pe.Fori(0, CHUNKS - 1) as c:
                adjacency(c + 1)
                output(c)
                first(c + 1)
                back(c, F_BANKS)
                second(c + 1)
                pe.wait_ge(x_ok, 4 * c + 4)
            output(CHUNKS - 1)

            def turn(bank, src):
                for q in range(SB):
                    last = TR(bank[:, q * 128:(q + 1) * 128], src(q), ident[:])
                return last

            def aggregate(s, b, par):
                for q in range(SB):
                    last = MM(PG[par][:, q * N:(q + 1) * N], nat[:, s, q, :],
                              an[:, bass.ds(b + q, 1), :].rearrange("p o n -> p (o n)"), start=True, stop=True)
                last.then_inc(G_ps, 1)

            def product(bank, w, g, xhi, xlo, start, stop):
                cols = slice(g * D, (g + 1) * D)
                MM(bank[:], w[:, 0, cols], xhi, start=start, stop=False)
                MM(bank[:], w[:, 0, cols], xlo, start=False, stop=False)
                return MM(bank[:], w[:, 1, cols], xhi, start=False, stop=stop)

            def enter(s):
                pe.wait_ge(x2_ok, s + 1)
                if s >= 2:
                    pe.wait_ge(hi_ok, s - 1)
                turn(X_BANKS[s % 2], lambda q: nat[:, s, q, :]).then_inc(X_ps, 1)
                if s >= 2:
                    pe.wait_ge(glo_ok, s - 1)
                aggregate(s, s * SB, s % 2)

            pe.wait_ge(a_ok, 1)
            enter(0)
            enter(1)
            back(CHUNKS - 1, F_BANKS_LAST)
            enter(2)
            enter(3)
            pe.wait_ge(hi_ok, SLOTS)
            pe.wait_ge(x_ok, 4 * CHUNKS - 1)
            for w in windows(pe):
                if w:
                    k, s = w.k, w.slot
                    xhi, xlo = hhi[:, s, :], hlo[:, s, :]
                    pe.wait_ge(hi_ok, k + 1)
                    pe.wait_ge(lo_ok, k + 1)
                    if w.turn:
                        pe.wait_ge(r_ok, k)
                    product(PR, wh, 0, xhi, xlo, True, False)
                    if w.turn:
                        pe.wait_ge(t1_ok, k)
                    product(PH, wh, 2, xhi, xlo, True, True)
                    if w.turn:
                        pe.wait_ge(z_ok, k)
                    product(PZ, wh, 1, xhi, xlo, True, False)
                    if w.out:
                        pe.wait_ge(h_ok, k - 1)
                        if w.out == "leave" and not (isinstance(w.visit, int) and w.visit == 0):
                            pe.wait_ge(sum_ok, w.visit)
                        if w.out == "step" and s == 2 and isinstance(w.l, int) and w.l == 0 and not (
                                isinstance(w.sg, int) and w.sg == 0):
                            pe.wait_ge(sum_ok, w.visit)
                        turn(PT, lambda q: hT[:, w.old, q * 128:(q + 1) * 128]).then_inc(T_ps if w.out == "step" else F_ps, 1)
                    if w.enter:
                        pe.wait_ge(a_ok, CHUNKS)
                        pe.wait_ge(x2_ok, w.visit + SLOTS + 1)
                        pe.wait_ge(hi_ok, k + 2)
                        turn(PX, lambda q: nat[:, w.old, q, :]).then_inc(X_ps, 1)
                    if s == 0:
                        pe.wait_ge(wcur_ok, w.sg * LAYERS + w.l + 1)
                    pe.wait_ge(ghi_ok, k + 1)
                    pe.wait_ge(glo_ok, k + 1)
                    xhi, xlo = ghi[:, s, :], glo[:, s, :]
                    product(PR, wcur, 0, xhi, xlo, False, True).then_inc(r_ps, 1)
                    if w.turn:
                        pe.wait_ge(c_ok, k)
                    product(PI, wcur, 2, xhi, xlo, True, True).then_inc(i_ps, 1)
                    product(PZ, wcur, 1, xhi, xlo, False, True).then_inc(z_ps, 1)
                    if w.feed:
                        if w.out == "step":
                            pe.wait_ge(nat_ok, w.turned + 1)
                        aggregate(w.old, w.batch, s % 2)
                else:
                    for slot, bank in ((SLOTS - 2, PT), (SLOTS - 1, PX)):
                        pe.wait_ge(h_ok, STEPS * CHUNKS - SLOTS + slot + 1)
                        pe.wait_ge(sum_ok, (CHUNKS - 1) * SLOTS + slot - 1 if bank is PX else B // SB - 2)
                        turn(bank, lambda q: hT[:, slot, q * 128:(q + 1) * 128]).then_inc(F_ps, 1)


_INS = ["x", "adj", "nodemask", "L0_gnn_W1", "L0_gnn_b1", "L0_gnn_W2", "L0_gnn_b2", "L0_gnn_fusion_w",
        "L1_gnn_weight", "L1_gnn_w_ih", "L1_gnn_w_hh", "L1_gnn_b_ih", "L1_gnn_b_hh"]


def kernel(**inputs):
    import numpy as _np
    import concourse.bacc as _bacc
    from concourse import mybir as _mybir
    from concourse.bass_utils import run_bass_kernel_spmd as _run

    nc = _bacc.Bacc("TRN2", target_bir_lowering=False, num_devices=1)
    arrays, args = {}, []
    for name in _INS:
        a = _np.ascontiguousarray(inputs[name])
        arrays[f"in_{name}_dram"] = a
        args.append(nc.dram_tensor(f"in_{name}_dram", a.shape, _mybir.dt.from_np(a.dtype), kind="ExternalInput").ap())
    args.append(nc.dram_tensor("out_0_dram", (B, N, D), _mybir.dt.float32, kind="ExternalOutput").ap())
    build(nc, *args)
    r = _run(nc, [arrays], core_ids=[0])
    return r.results[0]["out_0_dram"]
```
